# Optimizing a Trainium2 kernel written in Bass

```python
import numpy as np
import jax
import jax.numpy as jnp

def _softmax(x, axis=-1):
    return jax.nn.softmax(x, axis=axis)

def _gelu(x):
    return jax.nn.gelu(x, approximate=True)

def _silu(x):
    return jax.nn.silu(x)

def _sigmoid(x):
    return jax.nn.sigmoid(x)

def _layernorm(x, axis=-1, eps=1e-05):
    m = jnp.mean(x, axis=axis, keepdims=True)
    v = jnp.var(x, axis=axis, keepdims=True)
    return (x - m) / jnp.sqrt(v + eps)

def _scatter_add(tgt, idx, src, axis=0):
    return tgt.at[idx].add(src)

def _segment_sum(src, seg, n):
    return jax.ops.segment_sum(src, seg, n)
kernel_name = 'mk_gnn_ffn_d1_gnn_r8_2a9615'

def setup_inputs(seed: int=0):
    np.random.seed(seed)
    _w = jnp.asarray

    def _rec_inputs():
        import jax
        import jax.numpy as jnp
        _gk = jax.random.key(seed)
        x = -6.415e-05 + 1 * jax.random.normal(jax.random.fold_in(_gk, 1), (1250, 1024), jnp.float32)
        src = jax.random.randint(jax.random.fold_in(_gk, 2), (20000,), 0, 1250, jnp.int32)
        dst = jnp.minimum((1250 * jax.random.uniform(jax.random.fold_in(_gk, 3), (20000,)) ** 2.0).astype(jnp.int32), 9999)
        _o = jnp.argsort(dst, stable=True)
        src = src[_o]
        dst = dst[_o]
        edge_type_8 = jax.random.randint(jax.random.fold_in(_gk, 12), (20000,), 0, 8, jnp.int32)
        return (x, src, dst, edge_type_8)
    x, src, dst, edge_type_8 = _rec_inputs()

    def _L0_gnn_setup():
        import jax, jax.numpy as jnp
        import numpy as np
        N, D, R, E = (1250, 1024, 8, 10000)

        def _rgcn(x, edge_index, edge_type, weight, root, bias):
            src, dst = (edge_index[0], edge_index[1])
            msgs = x[src]
            out = x @ root + bias
            n = x.shape[0]
            for r in range(weight.shape[0]):
                mask = (edge_type == r).astype(x.dtype)
                sums = jax.ops.segment_sum(msgs * mask[:, None], dst, num_segments=n)
                cnt = jax.ops.segment_sum(mask, dst, num_segments=n)
                mean = sums / jnp.maximum(cnt, 1.0)[:, None]
                out = out + mean @ weight[r]
            return out
        key = jax.random.key(seed)
        ks = jax.random.split(key, 8)
        s = 1.0 / np.sqrt(D)
        x = jax.random.normal(ks[0], (N, D), dtype=jnp.float32)
        edge_index = jax.random.randint(ks[1], (2, E), 0, N, dtype=jnp.int64)
        edge_type = jax.random.randint(ks[2], (E,), 0, R, dtype=jnp.int64)
        weight = jax.random.normal(ks[3], (R, D, D), dtype=jnp.float32) * s
        root = jax.random.normal(ks[4], (D, D), dtype=jnp.float32) * s
        bias = jnp.zeros((D,), dtype=jnp.float32)
        w_gate = jax.random.normal(ks[5], (2 * D, D), dtype=jnp.float32) * (1.0 / np.sqrt(2 * D))
        b_gate = jnp.zeros((D,), dtype=jnp.float32)
        return {'x': x, 'edge_index': edge_index, 'edge_type': edge_type, 'weight': weight, 'root': root, 'bias': bias, 'w_gate': w_gate, 'b_gate': b_gate}
    _L0_gnn_all = _L0_gnn_setup()
    _L0_gnn_in = {k: v for k, v in _L0_gnn_all.items() if k in ('weight', 'root', 'bias', 'w_gate', 'b_gate')}
    del _L0_gnn_all

    def _L0_ffn_setup():
        import jax, jax.numpy as jnp
        import numpy as np
        EPS = 1e-05
        THRESHOLD = 0.7
        QMAX = 127.0

        def _fake_quant_act(x):
            scale = jnp.maximum(jnp.max(jnp.abs(x)), 1e-08) / QMAX
            q = jnp.round(jnp.clip(x / scale, -QMAX, QMAX)) * scale
            return x + jax.lax.stop_gradient(q - x)

        def _ternary_quant_weight(w):
            absw = jnp.abs(w)
            delta = THRESHOLD * jnp.mean(absw)
            mask = (absw > delta).astype(w.dtype)
            alpha = jnp.sum(absw * mask) / jnp.maximum(jnp.sum(mask), 1.0)
            wq = alpha * jnp.sign(w) * mask
            return w + jax.lax.stop_gradient(wq - w)
        key = jax.random.key(seed)
        k1, k2 = jax.random.split(key)
        B, S, D_IN, D_OUT = (4, 1024, 1024, 1024)
        x = jax.random.normal(k1, (B, S, D_IN), dtype=jnp.float32)
        weight = jax.random.normal(k2, (D_OUT, D_IN), dtype=jnp.float32) * np.sqrt(2.0 / D_IN)
        gamma = jnp.ones((D_IN,), dtype=jnp.float32)
        beta = jnp.zeros((D_IN,), dtype=jnp.float32)
        return {'x': x, 'weight': weight, 'gamma': gamma, 'beta': beta}
    _L0_ffn_all = _L0_ffn_setup()
    _L0_ffn_in = {k: v for k, v in _L0_ffn_all.items() if k in ('weight', 'gamma', 'beta')}
    del _L0_ffn_all
    return {'x': x, 'src': src, 'dst': dst, 'edge_type_8': edge_type_8, 'L0_gnn_weight': _L0_gnn_in['weight'], 'L0_gnn_root': _L0_gnn_in['root'], 'L0_gnn_bias': _L0_gnn_in['bias'], 'L0_gnn_w_gate': _L0_gnn_in['w_gate'], 'L0_gnn_b_gate': _L0_gnn_in['b_gate'], 'L0_ffn_weight': _L0_ffn_in['weight'], 'L0_ffn_gamma': _L0_ffn_in['gamma'], 'L0_ffn_beta': _L0_ffn_in['beta']}

def reference(x, src, dst, edge_type_8, L0_gnn_weight, L0_gnn_root, L0_gnn_bias, L0_gnn_w_gate, L0_gnn_b_gate, L0_ffn_weight, L0_ffn_gamma, L0_ffn_beta):
    import jax
    import jax.numpy as jnp

    def _L0_gnn_ref(x, edge_index, edge_type, weight, root, bias, w_gate, b_gate):
        import jax, jax.numpy as jnp
        import numpy as np
        N, D, R, E = (1250, 1024, 8, 10000)

        def _rgcn(x, edge_index, edge_type, weight, root, bias):
            src, dst = (edge_index[0], edge_index[1])
            msgs = x[src]
            out = x @ root + bias
            n = x.shape[0]
            for r in range(weight.shape[0]):
                mask = (edge_type == r).astype(x.dtype)
                sums = jax.ops.segment_sum(msgs * mask[:, None], dst, num_segments=n)
                cnt = jax.ops.segment_sum(mask, dst, num_segments=n)
                mean = sums / jnp.maximum(cnt, 1.0)[:, None]
                out = out + mean @ weight[r]
            return out
        u = _rgcn(x, edge_index, edge_type, weight, root, bias)
        z = jnp.concatenate([u, x], axis=1) @ w_gate + b_gate
        h = jnp.tanh(u) * z + x * (1.0 - z)
        return h

    def _L0_ffn_ref(x, weight, gamma, beta):
        import jax, jax.numpy as jnp
        import numpy as np
        EPS = 1e-05
        THRESHOLD = 0.7
        QMAX = 127.0

        def _fake_quant_act(x):
            scale = jnp.maximum(jnp.max(jnp.abs(x)), 1e-08) / QMAX
            q = jnp.round(jnp.clip(x / scale, -QMAX, QMAX)) * scale
            return x + jax.lax.stop_gradient(q - x)

        def _ternary_quant_weight(w):
            absw = jnp.abs(w)
            delta = THRESHOLD * jnp.mean(absw)
            mask = (absw > delta).astype(w.dtype)
            alpha = jnp.sum(absw * mask) / jnp.maximum(jnp.sum(mask), 1.0)
            wq = alpha * jnp.sign(w) * mask
            return w + jax.lax.stop_gradient(wq - w)
        mu = jnp.mean(x, axis=-1, keepdims=True)
        var = jnp.mean(jnp.square(x - mu), axis=-1, keepdims=True)
        xn = (x - mu) * jax.lax.rsqrt(var + EPS) * gamma + beta
        xq = _fake_quant_act(xn)
        wq = _ternary_quant_weight(weight)
        return jnp.einsum('bsi,oi->bso', xq, wq)
    edge_index = jnp.stack([src, dst])
    x = x + _L0_gnn_ref(_layernorm(x, axis=-1), edge_index, edge_type_8, L0_gnn_weight, L0_gnn_root, L0_gnn_bias, L0_gnn_w_gate, L0_gnn_b_gate)
    x = x + _L0_ffn_ref(_layernorm(x, axis=-1)[None], L0_ffn_weight, L0_ffn_gamma, L0_ffn_beta)[0]
    return x

_drawn_inputs = setup_inputs


def setup_inputs(seed=0):
    import zlib

    import numpy as np

    out = dict(_drawn_inputs(seed))
    spreads = {'L0_gnn_bias': (0.0, 0.1),
     'L0_gnn_b_gate': (0.0, 0.1),
     'L0_ffn_gamma': (1.0, 0.2),
     'L0_ffn_beta': (0.0, 0.1)}
    factors = {}
    for name, (base, spread) in spreads.items():
        noise = np.random.default_rng([zlib.crc32(name.encode()), seed]).standard_normal(out[name].shape)
        drawn = base * np.exp(spread * noise) if base else spread * noise
        out[name] = jnp.asarray(drawn.astype(out[name].dtype))
    for name, factor in factors.items():
        out[name] = (out[name] * factor).astype(out[name].dtype)
    return out
```

```python
from contextlib import ExitStack

import concourse.bass as bass
from concourse import mybir

F32, F32R = mybir.dt.float32, mybir.dt.float32r
F16, BF16, I32 = mybir.dt.float16, mybir.dt.bfloat16, mybir.dt.int32
ALU = mybir.AluOpType
ACT = mybir.ActivationFunctionType
AX = mybir.AxisListType

P = 128
N, D, R, E = 1250, 1024, 8, 20000
TP = 125
NT = N // TP
KT = D // P
H = 512
NH = D // H
EC = E // TP
PAIRS = 84
CH = 2 * PAIRS
AHEAD = 3
GS = 2 * AHEAD
CHX = CH + GS
STG = 4
NB = 4
LN_EPS = 1e-5
MAGIC = 1.5 * 2.0 ** 23
assert CH * P >= E + NT * (P - 1) - (P - 1) and EC % NB == 0


def build(nc, x, src, dst, etype, wall, bias, bgate, wffn, gamma, beta, out):
    ctx = ExitStack()
    with ctx:
        def sb(name, shape, dt):
            return ctx.enter_context(nc.sbuf_tensor(name, shape, dt))

        def sem(name):
            return ctx.enter_context(nc.semaphore(name))

        y_dram = [nc.dram_tensor(f"y_dram{j}", [R * N, H], F32, kind="Internal").ap() for j in range(NH)]
        rz_dram = nc.dram_tensor("rz_dram", [2 * NH * N, H], F32, kind="Internal").ap()
        agg_dram = nc.dram_tensor("agg_dram", [N, D], F32, kind="Internal").ap()
        inv_dram = nc.dram_tensor("inv_dram", [P * NT * R, 1], F32, kind="Internal").ap()
        tern_dram = nc.dram_tensor("tern_dram", [KT * P, D], BF16, kind="Internal").ap()
        y2_dram = nc.dram_tensor("y2_dram", [N, D], F32, kind="Internal").ap()
        xn_dram = nc.dram_tensor("xn_dram", [N, D], F32, kind="Internal").ap()

        xt_hi = sb("xt_hi", [P, KT, N], F32R)
        xt_lo = sb("xt_lo", [P, KT, N], F32R)
        w_hi = sb("w_hi", [P, 2, KT, H], F32R)
        w_lo = sb("w_lo", [P, 2, KT, H], F32R)
        w_stage = sb("w_stage", [P, STG, H], F32)
        agg = sb("agg", [P, NT, H], F32)
        gath = sb("gath", [P, GS, H], F32)
        msg_hi = sb("msg_hi", [P, 2, H], F32R)
        msg_lo = sb("msg_lo", [P, 2, H], F32R)
        onehot = sb("onehot", [P, 2, TP + 1], F32R)
        evict = sb("evict", [P, 2, H], F32)
        extra = sb("extra", [P, 2 * D], F32)
        idx_all = sb("idx_all", [P, 2, CHX], I32)
        low_s = sb("low_s", [P, CHX], F32)
        tile_i = sb("tile_i", [1, CHX], mybir.dt.int16)
        iota = sb("iota", [P, CH], F32)
        ident = sb("ident", [P, P], F32)
        ident_b = sb("ident_b", [P, P], BF16)
        idx_slot = sb("idx_slot", [P, AHEAD, 2, 2], I32)
        w_slot = sb("w_slot", [P, GS, 1], F32)
        mv = sb("mv", [P, NT, 2], F32)
        stats = sb("stats", [P, 4, 6], F32)
        sm = sb("sm", [P, 64], F32)
        amax = sb("amax", [P, NT], F32)

        def bank(name):
            return ctx.enter_context(nc.psum_tensor(name, [P, H], F32))
        yb = [bank("yb0"), bank("yb1")]
        ab = [bank("ab0"), bank("ab1")]
        tb = [bank("tb0"), bank("tb1")]
        perm_b, cnt_b = bank("perm_b"), bank("cnt_b")

        big = agg[:, :, :].rearrange("p t c -> p (t c)")
        gbig = gath[:, :, :].rearrange("p s c -> p (s c)")
        T = [big[:, i * D:(i + 1) * D] for i in range(5)]
        G = [gbig[:, i * D:(i + 1) * D] for i in range(3)]
        EV = evict[:, :, :].rearrange("p s c -> p (s c)")
        X0, X1 = extra[:, 0:D], extra[:, D:2 * D]

        s_const = sem("s_const")
        s_x = [sem("s_x0"), sem("s_x1")]
        s_dve = sem("s_dve")
        xl_ready = sem("xl_ready")
        tr_ready = sem("tr_ready")
        tr_hi = sem("tr_hi")
        tr_lo = sem("tr_lo")
        sd_ready = sem("sd_ready")
        sd_done = sem("sd_done")
        s_edges = sem("s_edges")
        oh_tile = sem("oh_tile")
        rank_ready = sem("rank_ready")
        rank_used = sem("rank_used")
        s_wf = [sem("s_wf0"), sem("s_wf1")]
        wf_abs = sem("wf_abs")
        wf_used = sem("wf_used")
        tern_ready = sem("tern_ready")
        tern_sq = sem("tern_sq")
        tern_t = sem("tern_t")
        tern_c = sem("tern_c")
        tern_st = [sem("tern_st0"), sem("tern_st1")]
        part_in = sem("part_in")
        part_out = sem("part_out")
        w_landed = [sem(f"w_landed{i}") for i in range(STG)]
        w_hi_done = sem("w_hi_done")
        w_lo_done = sem("w_lo_done")
        y_ready = sem("y_ready")
        y_free = sem("y_free")
        y_stored = [sem("y_stored0"), sem("y_stored1")]
        oh_ready = sem("oh_ready")
        oh_used = sem("oh_used")
        eq_ready = sem("eq_ready")
        perm_done = sem("perm_done")
        idx_ready = sem("idx_ready")
        s_inv = sem("s_inv")
        scratch_free = sem("scratch_free")
        agg_set = sem("agg_set")
        agg_out = sem("agg_out")
        icopy = sem("icopy")
        icopy_seen = sem("icopy_seen")
        g_landed = [sem(f"g_landed{i}") for i in range(GS)]
        gw_landed = [sem(f"gw_landed{i}") for i in range(GS)]
        msg_hi_done = sem("msg_hi_done")
        msg_lo_done = sem("msg_lo_done")
        agg_mm = sem("agg_mm")
        agg_added = sem("agg_added")
        d_in = [sem("d_in0"), sem("d_in1")]
        u_ready = sem("u_ready")
        th_done = sem("th_done")
        xl2_ready = sem("xl2_ready")
        base_ready = sem("base_ready")
        s_bc = sem("s_bc")
        gate_ready = sem("gate_ready")
        gate_taken = sem("gate_taken")
        y2_ready = sem("y2_ready")
        n_ready = sem("n_ready")
        xn_ready = sem("xn_ready")
        xn_maxed = sem("xn_maxed")
        e1_out = [sem("e1_out0"), sem("e1_out1")]
        gm_in = sem("gm_in")
        gm_out = sem("gm_out")
        s_tern = sem("s_tern")
        e2_in = [sem("e2_in0"), sem("e2_in1")]
        q_ready = sem("q_ready")
        qt_ready = sem("qt_ready")
        qt_done = sem("qt_done")
        f_ready = sem("f_ready")
        f_done = sem("f_done")
        o_out = [sem("o_out0"), sem("o_out1")]

        ex = [extra[0:TP, i * EC:(i + 1) * EC] for i in range(12)]
        srcf, dstf, typf, tile_a, tile_b, lowf, bfld, k80, pcf, plf = ex[2:12]
        ei = [ex[i].bitcast(I32) for i in (0, 1)]
        C16 = NT * EC
        cumT, cumI = big[:, 0:C16], big[:, C16:2 * C16]
        rankV = big[0:TP, 2 * C16:3 * C16]
        g16 = gbig[0:TP, :].bitcast(BF16)
        oh_t, low_tri, ones_b = g16[:, 0:C16], g16[:, C16:C16 + 128], g16[:, C16 + 128:C16 + 256]
        big16 = big[0:TP, :].bitcast(F16)
        OHW = NB * (P + 2 * CH + CH + TP + 3 + NT * R)

        def batch_slot(s):
            at, res = s * OHW, []
            for w in (P, 2 * CH, CH, TP + 3, NT * R):
                res.append(big16[:, at:at + NB * w].rearrange("p (c w) -> p c w", c=NB))
                at += NB * w
            return res
        batches = [batch_slot(0), batch_slot(1)]

        tern_v = [gbig.bitcast(BF16)[:, i * D:(i + 1) * D] for i in range(6)] + \
                 [T[4].bitcast(BF16)[:, i * D:(i + 1) * D] for i in range(2)]
        tern_w = big[:, D:5 * D].bitcast(BF16).rearrange("p (o k c) -> p o k c", o=KT, k=KT)

        A = [T[0], G[0]]
        Rr = [T[1], T[2]]
        Xx = [T[3], T[4]]
        Zz = [G[1], G[2]]
        exb = extra[:, :].bitcast(BF16)
        Qb = [exb[:, 0:D], exb[:, D:2 * D]]
        qT = [exb[:, 2 * D:2 * D + KT * TP].rearrange("p (k n) -> p k n", k=KT),
              exb[:, 3 * D:3 * D + KT * TP].rearrange("p (k n) -> p k n", k=KT)]

        cntt, capt, base, delta_t, cap_i, tmp10 = (sm[:, 10 * i:10 * i + 10] for i in range(6))
        smc = lambda i: sm[:, 60 + i:61 + i]
        asum = sb("asum", [P, 2 * KT + 8], F32)
        thr, nthr, alpha = asum[:, 2 * KT:2 * KT + 1], asum[:, 2 * KT + 1:2 * KT + 2], asum[:, 2 * KT + 2:2 * KT + 3]
        tot_s, tot_n = asum[:, 2 * KT + 3:2 * KT + 4], asum[:, 2 * KT + 4:2 * KT + 5]
        both = asum[:, 2 * KT + 3:2 * KT + 5]
        psums = asum[:, 2 * KT + 5:2 * KT + 7]
        gmx, qinv = smc(0), smc(1)
        outscale, gms = smc(2), smc(3)

        rows = lambda ap, t: ap[t * TP:(t + 1) * TP, :]
        rz_v = rz_dram.rearrange("(u n) c -> n u c", u=2 * NH)
        f = lambda ap: ap.bitcast(F32)

        pairs_b1 = [2 if m == 0 else 1 for m in range(2 * NT)]
        pairs_c = [3 if m in (0, NT) else 2 for m in range(2 * NT)]
        LOOPS = (
            (0, 2, None, None), (4, 2, None, None), (8, 4, pairs_b1, 0), (16, 2, pairs_c, 1))

        block = ctx.enter_context(nc.Block())

        def with_pairs(first, pairs, i, s, m):
            if pairs is None:
                return []
            per, at = sum(pairs), sum(pairs[:s * NT + m])
            return [(i * per + at + q, (at + q) % AHEAD) for q in range(pairs[s * NT + m])]

        def store_e1(sp, t):
            sp.wait_ge(y2_ready, t + 1)
            sp.dma_start(rows(y2_dram, t), Zz[t % 2][0:TP, :]).then_inc(e1_out[t % 2], 16)
            sp.wait_ge(xn_maxed, t + 1)
            sp.dma_start(rows(xn_dram, t), A[t % 2][0:TP, :]).then_inc(e1_out[t % 2], 16)

        def store_out(sp, t):
            sp.wait_ge(f_done, 2 * (t + 1))
            sp.dma_start(rows(out, t), Zz[t % 2][0:TP, :]).then_inc(o_out[t % 2], 16)

        def lo_half(dve, n0, t):
            for h in range(2):
                dve.wait_ge(tr_hi, n0 + h + 1)
                dst3 = (xt_lo[:, 4 * h:4 * h + 4, t * TP:(t + 1) * TP])
                hi3 = f(xt_hi[:, 4 * h:4 * h + 4, t * TP:(t + 1) * TP])
                dve.tensor_tensor(dst3, tb[h][:, 0:4 * TP].rearrange("p (k n) -> p k n", k=4), hi3,
                                  ALU.subtract).then_inc(tr_lo, 1)

        @block.sync
        def _(sp):
            def load_w(g, k):
                sp.dma_start(w_stage[:, k % STG, :], wall[bass.ds(g * P, P), :] if not isinstance(g, int)
                             else wall[g * P:(g + 1) * P, :]).then_inc(w_landed[k % STG], 16)

            for t in range(2):
                sp.dma_start(T[t][0:TP, :], rows(x, t)).then_inc(s_x[t], 16)
            for e, (a, t) in enumerate(((src, ei[0]), (dst, ei[1]))):
                sp.dma_start(t, a.rearrange("(p c) -> p c", p=TP)).then_inc(s_edges, 16)
            for k in range(STG):
                load_w(k, k)
            for t in range(2, NT):
                sp.wait_ge(xl_ready, t - 1)
                sp.dma_start(T[t % 2][0:TP, :], rows(x, t)).then_inc(s_x[t % 2], 16)
            sp.wait_ge(scratch_free, 1)
            sp.dma_start(ei[0], etype.rearrange("(p c) -> p c", p=TP)).then_inc(s_edges, 16)
            for k in range(STG, KT):
                sp.wait_ge(w_lo_done, k - STG + 1)
                load_w(k, k)
            sp.wait_ge(scratch_free, 2)
            for o in range(2 * KT):
                if o >= 2:
                    sp.wait_ge(wf_used, o - 1)
                sp.dma_start(T[o % 2], wffn[(o % KT) * P:(o % KT + 1) * P, :]).then_inc(s_wf[o % 2], 16)

            def units(first, iters, table, table_first):
                with sp.Fori(0, iters) as i:
                    for s in range(2):
                        u = i * 2 + (first + s)
                        for m in range(NT):
                            if m < KT:
                                sp.wait_ge(w_lo_done, u * KT + (KT + m - STG + 1))
                                sp.dma_start(w_stage[:, m % STG, :], wall[bass.ds(u * (KT * P) + (KT + m) * P, P), :]
                                             ).then_inc(w_landed[m % STG], 16)
                            sp.wait_ge(y_free, u * NT + (m + 3))
                            sp.dma_start(table[bass.ds(i * (2 * N) + ((first - table_first + s) * N + m * TP), TP), :],
                                         evict[0:TP, m % 2, :]).then_inc(y_stored[m % 2], 16)

            units(0, 2, y_dram[0], 0)
            for o in range(KT):
                sp.wait_ge(tern_c, o + 1)
                sp.dma_start(tern_dram[o * P:(o + 1) * P, :], T[o % 2].bitcast(BF16)[:, 0:D]).then_inc(tern_st[o % 2], 16)
            units(4, 2, y_dram[0], 0)
            units(8, 4, y_dram[1], 8)
            units(16, 2, rz_dram, 16)
            for k in range(KT):
                sp.wait_ge(w_lo_done, 21 * KT + k - STG + 1)
                load_w(21 * KT + k, k)
            sp.wait_ge(agg_out, 32)
            sp.wait_ge(s_bc, 48)
            for q in range(2):
                sp.wait_ge(y_stored[q], 16 * 20 * NT // 2)
            for t in range(NT):
                s = t % 2
                if t >= 2:
                    sp.wait_ge(e1_out[s], 32 * (t // 2))
                sp.dma_start(A[s][0:TP, :], rows(agg_dram, t)).then_inc(d_in[s], 16)
                sp.dma_start(Rr[s][0:TP, :].rearrange("p (u c) -> p u c", u=2), rz_v[t * TP:(t + 1) * TP, 0:2, :]
                             ).then_inc(d_in[s], 16)
                sp.dma_start(Xx[s][0:TP, :], rows(x, t)).then_inc(d_in[s], 16)
                sp.dma_start(Zz[s][0:TP, :].rearrange("p (u c) -> p u c", u=2), rz_v[t * TP:(t + 1) * TP, 2:4, :]
                             ).then_inc(d_in[s], 16)
                if t >= 1:
                    store_e1(sp, t - 1)
            store_e1(sp, NT - 1)
            for q in range(2):
                sp.wait_ge(e1_out[q], 32 * NT // 2)
            sp.dma_start(tern_w.rearrange("p o k c -> p o (k c)"), tern_dram.rearrange("(o p) c -> p o c", p=P)).then_inc(s_tern, 16)
            for t in range(NT):
                s = t % 2
                if t >= 2:
                    sp.wait_ge(o_out[s], 16 * (t // 2))
                    sp.wait_ge(q_ready, t - 1)
                sp.dma_start(A[s][0:TP, :], rows(xn_dram, t)).then_inc(e2_in[s], 16)
                sp.dma_start(Zz[s][0:TP, :], rows(y2_dram, t)).then_inc(e2_in[s], 16)
                if t >= 1:
                    store_out(sp, t - 1)
            store_out(sp, NT - 1)
            for q in range(2):
                sp.wait_ge(o_out[q], 16 * NT // 2)

        @block.tensor
        def _(pe):
            def transpose_tile(src_tile, n0, hold):
                for h in range(2):
                    if n0 + h >= 2:
                        pe.wait_ge(tr_lo, n0 + h - 1)
                    for q in range(4):
                        ins = pe.transpose(tb[h][:, q * TP:(q + 1) * TP],
                                           src_tile[0:TP, (4 * h + q) * P:(4 * h + q + 1) * P], ident[0:TP, 0:TP])
                    ins.then_inc(tr_ready, 1)

            pe.wait_ge(s_const, 6)
            for t in range(NT):
                pe.wait_ge(xl_ready, t + 1)
                transpose_tile(T[2 + t % 2], 2 * t, None)

            pe.wait_ge(oh_tile, 1)
            w2 = 2 * EC
            for q in range(NT // 2):
                for n, tri, m in ((2 * q, ones_b, P), (2 * q + 1, low_tri, TP)):
                    if n >= 2:
                        pe.wait_ge(rank_used, n - 1)
                    pe.matmul(ab[n % 2][0:m, 0:w2], tri[:, 0:m], oh_t[:, q * w2:(q + 1) * w2], start=True, stop=True
                              ).then_inc(rank_ready, 1)

            def chunk(c, half, s2):
                n = c + half * CH
                pe.wait_ge(msg_lo_done, n + 1)
                pe.wait_ge(agg_added, n + 1)
                pe.matmul(ab[s2][0:TP, :], onehot[:, s2, 0:TP], msg_hi[:, s2, :], start=True, stop=False)
                pe.matmul(ab[s2][0:TP, :], onehot[:, s2, 0:TP], msg_lo[:, s2, :], start=False, stop=True
                          ).then_inc(agg_mm, 1)

            def sort_batch(b, s):
                ohl, rhs, _, ohlow, oh80 = batches[s]
                pe.wait_ge(oh_ready, b + 1)
                for c in range(NB):
                    pe.matmul(perm_b[:, 0:2 * CH], ohl[:, c, :], rhs[:, c, :], start=False, stop=False, skip_group_check=True)
                    ins = pe.matmul(cnt_b[0:TP, 0:NT * R], ohlow[:, c, 0:TP], oh80[:, c, :], start=False, stop=False,
                                    skip_group_check=True)
                ins.then_inc(oh_used, 1)

            def unit_tile(u, s, m, chunks):
                todo = list(chunks)
                pe.wait_ge(y_free, u * NT + (m + 1))
                for k in range(KT):
                    if m == 0:
                        pe.wait_ge(w_lo_done, u * KT + (k + 1))
                    xh, xl = xt_hi[:, k, m * TP:(m + 1) * TP], xt_lo[:, k, m * TP:(m + 1) * TP]
                    o = yb[m % 2][0:TP, :]
                    pe.matmul(o, xh, w_hi[:, s, k, :], start=k == 0, stop=False)
                    pe.matmul(o, xh, w_lo[:, s, k, :], start=False, stop=False)
                    ins = pe.matmul(o, xl, w_hi[:, s, k, :], start=False, stop=k == KT - 1)
                    if k == KT - 1:
                        ins.then_inc(y_ready, 1)
                    while todo and k >= KT - len(todo):
                        chunk(*todo.pop(0))

            pe.wait_ge(tr_lo, 2 * NT)
            for n, (first, iters, pairs, half) in enumerate(LOOPS):
                if n == 1:
                    for o in range(KT):
                        pe.wait_ge(tern_ready, o + 1)
                        if o >= 2:
                            pe.wait_ge(tern_c, o - 1)
                        tbb = tb[o % 2][:, :].bitcast(BF16)
                        for k in range(KT):
                            ins = pe.transpose(tbb[:, k * P:(k + 1) * P], tern_v[o][:, k * P:(k + 1) * P], ident_b[:, :])
                        ins.then_inc(tern_t, 1)
                    pe.wait_ge(s_const, 7)
                    z = idx_all[:, :, :].rearrange("p a c -> p (a c)").bitcast(F16)
                    pe.matmul(perm_b[:, 0:2 * CH], z[:, 0:P], z[:, 0:2 * CH], start=True, stop=False, skip_group_check=True)
                    pe.matmul(cnt_b[0:TP, 0:NT * R], z[:, 0:TP], z[:, 0:NT * R], start=True, stop=False, skip_group_check=True)
                with pe.Fori(0, iters) as i:
                    for s in range(2):
                        for m in range(NT):
                            u = i * 2 + (first + s)
                            cs = [(2 * p + e, half, e) for p, _ in with_pairs(first, pairs, i, s, m) for e in range(2)]
                            unit_tile(u, s, m, cs)
                            if n == 1:
                                sort_batch(i * (2 * NT) + (s * NT + m), m % 2)
                if n == 1:
                    z = idx_all[:, :, :].rearrange("p a c -> p (a c)").bitcast(F16)
                    pe.matmul(perm_b[:, 0:2 * CH], z[:, 0:P], z[:, 0:2 * CH], start=False, stop=True, skip_group_check=True)
                    pe.matmul(cnt_b[0:TP, 0:NT * R], z[:, 0:TP], z[:, 0:NT * R], start=False, stop=True,
                              skip_group_check=True).then_inc(perm_done, 1)

            pe.wait_ge(y_ready, 20 * NT)
            for t in range(NT + 1):
                if t < NT:
                    pe.wait_ge(u_ready, t + 1)
                    transpose_tile(A[t % 2], 2 * NT + 2 * t, None)
                if t >= 1:
                    m = t - 1
                    pe.wait_ge(tr_lo, 2 * NT + 2 * t)
                    pe.wait_ge(w_lo_done, 22 * KT)
                    for j in range(NH):
                        if t >= 2:
                            pe.wait_ge(gate_taken, 2 * (m - 1) + j + 1)
                        else:
                            pe.wait_ge(y_free, 20 * NT + 2)
                        for k in range(KT):
                            xh, xl = xt_hi[:, k, m * TP:(m + 1) * TP], xt_lo[:, k, m * TP:(m + 1) * TP]
                            pe.matmul(yb[j][0:TP, :], xh, w_hi[:, j, k, :], start=k == 0, stop=False)
                            pe.matmul(yb[j][0:TP, :], xh, w_lo[:, j, k, :], start=False, stop=False)
                            ins = pe.matmul(yb[j][0:TP, :], xl, w_hi[:, j, k, :], start=False, stop=k == KT - 1)
                        ins.then_inc(gate_ready, 1)
            for t in range(NT + 1):
                if t < NT:
                    pe.wait_ge(q_ready, t + 1)
                    if t >= 2:
                        pe.wait_ge(qt_done, t - 1)
                    else:
                        pe.wait_ge(tr_lo, 4 * NT)
                    tbb = tb[t % 2][:, :].bitcast(BF16)
                    for k in range(KT):
                        ins = pe.transpose(tbb[:, k * P:k * P + TP],
                                           Qb[t % 2][0:TP, k * P:(k + 1) * P], ident_b[0:TP, 0:TP])
                    ins.then_inc(qt_ready, 1)
                if t >= 1:
                    m = t - 1
                    pe.wait_ge(qt_done, t)
                    if m == 0:
                        pe.wait_ge(s_tern, 16)
                    for j in range(NH):
                        if m >= 1:
                            pe.wait_ge(f_done, 2 * (m - 1) + j + 1)
                        else:
                            pe.wait_ge(gate_taken, 2 * NT)
                        for k in range(KT):
                            ins = pe.matmul(yb[j][0:TP, :], qT[m % 2][:, k, :], tern_w[:, 4 * j:4 * j + 4, k, :],
                                            start=k == 0, stop=k == KT - 1)
                        ins.then_inc(f_ready, 1)

        @block.scalar
        def _(act):
            def sqrt_var(n, ap):
                act.wait_ge(sd_ready, n + 1)
                act.activation(ap, ap, ACT.Sqrt).then_inc(sd_done, 1)

            def tr_half(n, t, h):
                act.wait_ge(tr_ready, n + 1)
                act.activation(xt_hi[:, 4 * h:4 * h + 4, t * TP:(t + 1) * TP],
                               tb[h][:, 0:4 * TP].rearrange("p (k n) -> p k n", k=4), ACT.Copy).then_inc(tr_hi, 1)

            def w_split_hi(g_wait, s, k):
                act.wait_ge(w_landed[k % STG], g_wait)
                act.activation(w_hi[:, s, k, :], w_stage[:, k % STG, :], ACT.Copy).then_inc(w_hi_done, 1)

            act.sem_inc(y_free, 2)
            for t in range(NT):
                sqrt_var(t, mv[0:TP, t, 1:2])
                if t >= 1:
                    for h in range(2):
                        tr_half(2 * (t - 1) + h, t - 1, h)
            for h in range(2):
                tr_half(2 * (NT - 1) + h, NT - 1, h)
            for k in range(KT):
                w_split_hi(16 * (k // STG + 1), 0, k)
            for o in range(KT):
                act.wait_ge(s_wf[o % 2], 16 * (o // 2 + 1))
                if o >= 1:
                    act.wait_ge(wf_used, o)
                act.activation(T[2], T[o % 2], ACT.Abs, accum_out=asum[:, o:o + 1]).then_inc(wf_used, 1)
            for o in range(KT):
                act.wait_ge(tern_ready, o + 1)
                act.wait_ge(wf_used, KT)
                if o >= 1:
                    act.wait_ge(tern_sq, o)
                act.activation(T[2], tern_v[o], ACT.Square, accum_out=asum[:, KT + o:KT + o + 1]).then_inc(tern_sq, 1)

            def units(n, first, iters, pairs, half):
                with act.Fori(0, iters) as i:
                    for s in range(2):
                        u = i * 2 + (first + s)
                        for m in range(NT):
                            if 1 <= m <= KT:
                                k = m - 1
                                if k == 0:
                                    act.wait_ge(y_ready, u * NT)
                                w_split_hi(u * 32 + 16 * (2 + k // STG + 1), 1 - s, k)
                            if pairs is not None:
                                per, at0 = sum(pairs), sum(pairs[:s * NT + m])
                                for q in range(pairs[s * NT + m]):
                                    at = at0 + q
                                    for e in range(2):
                                        s6 = 2 * (at % AHEAD) + e
                                        landed = i * (16 * per // AHEAD) + 16 * (at // AHEAD + 1 + half * CHX // GS)
                                        act.wait_ge(g_landed[s6], landed)
                                        act.wait_ge(gw_landed[s6], landed)
                                        act.wait_ge(agg_mm, i * (2 * per) + (2 * at + e + half * CH + 1))
                                        act.activation(msg_hi[:, e, :], gath[:, s6, :], ACT.Copy,
                                                       scale=w_slot[:, s6, :]).then_inc(msg_hi_done, 1)
                            act.wait_ge(y_ready, u * NT + (m + 1))
                            act.wait_ge(y_stored[m % 2], u * (16 * NT // 2) + 16 * (m // 2))
                            act.activation(evict[0:TP, m % 2, :], yb[m % 2][0:TP, :], ACT.Copy).then_inc(y_free, 1)

            for n, loop in enumerate(LOOPS):
                if n == 1:
                    for o in range(KT):
                        act.wait_ge(tern_t, o + 1)
                        if o >= 2:
                            act.wait_ge(tern_st[o % 2], 16 * (o // 2))
                        act.activation(T[o % 2].bitcast(BF16)[:, 0:D], tb[o % 2][:, :].bitcast(BF16), ACT.Copy).then_inc(tern_c, 1)
                units(n, *loop)
            act.wait_ge(y_ready, 20 * NT)
            for k in range(KT):
                w_split_hi(16 * (21 * 2 + k // STG + 1), 1, k)
            for t in range(NT + 1):
                if t < NT:
                    s = t % 2
                    act.wait_ge(u_ready, t + 1)
                    act.activation(Rr[s][0:TP, :], A[s][0:TP, :], ACT.Tanh).then_inc(th_done, 1)
                    for h in range(2):
                        tr_half(2 * NT + 2 * t + h, t, h)
                if t >= 1:
                    sqrt_var(NT + 2 * (t - 1), sm[0:TP, 0:1])
                    sqrt_var(NT + 2 * (t - 1) + 1, sm[0:TP, 0:1])
            for t in range(NT):
                act.wait_ge(qt_ready, t + 1)
                if t >= 2:
                    act.wait_ge(f_ready, 2 * (t - 1))
                act.activation(qT[t % 2], tb[t % 2][:, :].bitcast(BF16).rearrange("p (k n) -> p k n", k=KT)[:, :, 0:TP],
                               ACT.Copy).then_inc(qt_done, 1)

        @block.vector
        def _(dve):
            steps = [0]

            def done(ins):
                steps[0] += 1
                ins.then_inc(s_dve, 1)
                dve.wait_ge(s_dve, steps[0])

            dve.sem_inc(agg_added, 2)
            n_sd = [0]

            def row_stats(tile, mean_rstd, st):
                for h in range(2):
                    done(dve.bn_stats(stats[0:TP, st + h, :], tile[:, h * H:(h + 1) * H]))
                done(dve.bn_aggr(mean_rstd, stats[0:TP, st:st + 2, :].rearrange("p a b -> p (a b)")))

            for t in range(NT):
                dve.wait_ge(s_x[t % 2], 16 * (t // 2 + 1))
                xin, xl = T[t % 2][0:TP, :], T[2 + t % 2][0:TP, :]
                row_stats(xin, mv[0:TP, t, :], 2 * (t % 2))
                dve.tensor_scalar(mv[0:TP, t, 1:2], mv[0:TP, t, 1:2], LN_EPS, None, ALU.add).then_inc(sd_ready, 1)
                if t >= 1:
                    lo_half(dve, 2 * (t - 1), t - 1)
                dve.wait_ge(sd_done, t + 1)
                done(dve.reciprocal(mv[0:TP, t, 1:2], mv[0:TP, t, 1:2]))
                if t >= 2:
                    dve.wait_ge(tr_ready, 2 * (t - 1))
                dve.tensor_scalar(xl, xin, mv[0:TP, t, 0:1], mv[0:TP, t, 1:2], ALU.subtract, ALU.mult).then_inc(xl_ready, 1)
            lo_half(dve, 2 * (NT - 1), NT - 1)

            dve.wait_ge(s_edges, 32)
            done(dve.tensor_copy(srcf, ei[0]))
            dve.tensor_copy(dstf, ei[1]).then_inc(scratch_free, 1)
            dve.wait_ge(scratch_free, 1)
            done(dve.tensor_scalar(tile_a, dstf, float(TP), None, ALU.is_ge))
            cur, nxt = tile_a, tile_b
            for t in range(2, NT):
                done(dve.scalar_tensor_tensor(nxt, dstf, float(t * TP), cur, ALU.is_ge, ALU.add))
                cur, nxt = nxt, cur
            tl = cur
            done(dve.scalar_tensor_tensor(lowf, tl, -float(TP), dstf, ALU.mult, ALU.add))
            dve.wait_ge(s_const, 6)
            for t in range(NT):
                ins = dve.tensor_scalar(oh_t[:, t * EC:(t + 1) * EC], tl, float(t), None, ALU.is_equal)
            ins.then_inc(oh_tile, 1)
            dve.wait_ge(s_edges, 48)
            done(dve.tensor_copy(typf, ei[0]))
            done(dve.scalar_tensor_tensor(k80, tl, float(R), typf, ALU.mult, ALU.add))
            done(dve.scalar_tensor_tensor(bfld, typf, float(P), lowf, ALU.mult, ALU.add))
            done(dve.tensor_scalar(bfld, bfld, 1.0, None, ALU.add))
            w2 = 2 * EC
            for q in range(NT // 2):
                for n, dest, m in ((2 * q, cumT, P), (2 * q + 1, rankV, TP)):
                    dve.wait_ge(rank_ready, n + 1)
                    dve.tensor_copy(dest[:, q * w2:(q + 1) * w2], ab[n % 2][0:m, 0:w2]).then_inc(rank_used, 1)
            dve.wait_ge(rank_used, NT)
            done(dve.tensor_tensor(rankV, rankV, cumT[0:TP, :], ALU.subtract))
            done(dve.memset(cumI, 0.0))
            done(dve.tensor_tensor_scan(cumI, cumI, cumT, 0.0, ALU.add, ALU.add))
            done(dve.tensor_tensor(rankV, rankV, cumI[0:TP, :], ALU.add))
            ends = cumI.rearrange("p (t c) -> p t c", t=NT)[:, :, EC - 1]
            done(dve.tensor_copy(tmp10, ends))
            done(dve.tensor_copy(cntt[:, 0:1], tmp10[:, 0:1]))
            done(dve.tensor_tensor(cntt[:, 1:NT], tmp10[:, 1:NT], tmp10[:, 0:NT - 1], ALU.subtract))
            done(dve.tensor_scalar(cap_i.bitcast(I32), cntt, float(P - 1), None, ALU.add))
            done(dve.tensor_scalar(cap_i.bitcast(I32), cap_i.bitcast(I32), -P, None, ALU.bitwise_and))
            done(dve.tensor_copy(capt, cap_i.bitcast(I32)))
            done(dve.memset(base, 0.0))
            done(dve.tensor_tensor_scan(base, base, capt, 0.0, ALU.add, ALU.add))
            done(dve.tensor_tensor(base, base, capt, ALU.subtract))
            done(dve.tensor_tensor(delta_t, base, tmp10, ALU.subtract))
            done(dve.tensor_tensor(delta_t, delta_t, cntt, ALU.add))
            v3 = rankV.rearrange("p (t c) -> p t c", t=NT)
            o3 = oh_t.rearrange("p (t c) -> p t c", t=NT)
            done(dve.tensor_tensor(v3, v3, delta_t[0:TP, :].unsqueeze(2).to_broadcast([TP, NT, EC]), ALU.add))
            done(dve.tensor_tensor(rankV, rankV, oh_t, ALU.mult))
            done(dve.tensor_reduce(pcf, rankV.rearrange("p (t c) -> p c t", t=NT), AX.X, ALU.add))
            pos_i, lane_i = tile_a.bitcast(I32), tile_b.bitcast(I32)
            done(dve.tensor_copy(pos_i, pcf))
            done(dve.tensor_scalar(lane_i, pos_i, P - 1, None, ALU.bitwise_and))
            done(dve.tensor_copy(plf, lane_i))
            done(dve.tensor_scalar(lane_i, pos_i, 7, None, ALU.arith_shift_right))
            done(dve.tensor_copy(pcf, lane_i))
            ca, cb = cumT[:, 0:CHX], cumT[:, CHX:2 * CHX]
            i128 = cumT[:, 2 * CHX:2 * CHX + CH]
            done(dve.tensor_scalar(i128, iota[:, :], float(P), None, ALU.mult))
            done(dve.memset(ca, float(NT - 1)))
            done(dve.memset(cb, float(NT - 1)))
            done(dve.tensor_scalar(ca[:, 0:CH], i128, base[:, 1:2], None, ALU.is_ge))
            for t in range(2, NT):
                done(dve.scalar_tensor_tensor(cb[:, 0:CH], i128, base[:, t:t + 1], ca[:, 0:CH], ALU.is_ge, ALU.add))
                ca, cb = cb, ca
            done(dve.tensor_copy(tile_i[0:1, :], ca[0:1, :]))
            dve.tensor_scalar(low_s[:, :], ca, float(R), None, ALU.mult).then_inc(scratch_free, 1)

            dve.wait_ge(wf_used, KT)
            done(dve.tensor_reduce(tot_s, asum[:, 0:KT], AX.X, ALU.add))
            dve.memset(tot_n, 0.0).then_inc(part_in, 1)
            dve.wait_ge(part_out, 1)
            done(dve.tensor_scalar(thr, psums[:, 0:1], 1.0 / (D * D), None, ALU.mult))
            done(dve.tensor_scalar(thr, thr, 0.7, None, ALU.mult))
            done(dve.tensor_scalar(nthr, thr, -1.0, None, ALU.mult))
            for o in range(KT):
                dve.wait_ge(s_wf[o % 2], 16 * (KT // 2 + o // 2 + 1))
                w = T[o % 2]
                done(dve.tensor_scalar(T[3], w, nthr, None, ALU.is_lt))
                dve.scalar_tensor_tensor(tern_v[o], w, thr, T[3], ALU.is_gt, ALU.subtract).then_inc(tern_ready, 1)
                dve.wait_ge(tern_ready, o + 1)
                dve.scalar_tensor_tensor(T[3], w, 1.0, tern_v[o], ALU.mult, ALU.mult,
                                         accum_out=asum[:, o:o + 1]).then_inc(wf_used, 1)
                dve.wait_ge(wf_used, KT + o + 1)
            dve.wait_ge(tern_sq, KT)
            done(dve.tensor_reduce(tot_s, asum[:, 0:KT], AX.X, ALU.add))
            dve.tensor_reduce(tot_n, asum[:, KT:2 * KT], AX.X, ALU.add).then_inc(part_in, 1)
            dve.wait_ge(part_out, 2)
            done(dve.tensor_scalar(tot_n, psums[:, 1:2], 1.0, None, ALU.max))
            done(dve.reciprocal(tot_n, tot_n))
            done(dve.tensor_tensor(alpha, psums[:, 0:1], tot_n, ALU.mult))

            for q in range(2):
                dve.wait_ge(tern_st[q], 16 * KT // 2)
            dve.sem_inc(oh_used, 2)

            def bc(ap, w):
                return ap.unsqueeze(2).to_broadcast([TP, NB, w])

            def io(w):
                return iota[0:TP, 0:w].unsqueeze(1).to_broadcast([TP, NB, w])

            with dve.Fori(0, 2) as i:
                for b20 in range(2 * NT):
                    b = i * (2 * NT) + b20
                    ohl, rhs, eq, ohlow, oh80 = batches[b20 % 2]
                    cols = lambda ap: ap[:, bass.ds(b * NB, NB)]
                    dve.wait_ge(oh_used, b + 1)
                    dve.tensor_tensor(eq, io(CH), bc(cols(pcf), CH), ALU.is_equal).then_inc(eq_ready, 1)
                    dve.tensor_tensor(ohl, io(P), bc(cols(plf), P), ALU.is_equal)
                    dve.tensor_tensor(ohlow, io(P), bc(cols(lowf), P), ALU.is_equal)
                    dve.tensor_tensor(oh80, io(NT * R), bc(cols(k80), NT * R), ALU.is_equal)
                    dve.wait_ge(eq_ready, b + 1)
                    dve.tensor_tensor(rhs[:, :, 0:CH], eq, bc(cols(srcf), CH), ALU.mult)
                    dve.tensor_tensor(rhs[:, :, CH:2 * CH], eq, bc(cols(bfld), CH), ALU.mult).then_inc(oh_ready, 1)

            dve.wait_ge(perm_done, 1)
            sv = big[:, 0:4 * CH].rearrange("p (a c) -> p a c", a=4)
            tabs = big[:, 2048:2048 + NT * R]
            tabs2 = big[:, 2560:2560 + CH]
            ti = sv[:, 2, :].bitcast(I32)
            tj = sv[:, 3, :].bitcast(I32)
            done(dve.memset(tabs, 0.0))
            done(dve.tensor_scalar(tabs[0:TP, :], cnt_b[0:TP, 0:NT * R], 1.0, None, ALU.max))
            dve.reciprocal(tabs[0:TP, :], tabs[0:TP, :]).then_inc(idx_ready, 1)
            done(dve.tensor_scalar(ti, perm_b[:, CH:2 * CH], -1.0, None, ALU.add))
            done(dve.tensor_scalar(tj, ti, P - 1, None, ALU.bitwise_and))
            low = tabs2
            done(dve.tensor_copy(low, tj))
            done(dve.tensor_scalar(tj, ti, 7, None, ALU.arith_shift_right))
            done(dve.tensor_copy(sv[:, 0, :], tj))
            done(dve.tensor_scalar(sv[:, 0, :], sv[:, 0, :], 0.0, None, ALU.max))
            done(dve.scalar_tensor_tensor(idx_all[:, 0, 0:CH], sv[:, 0, :], float(N), perm_b[:, 0:CH], ALU.mult, ALU.add))
            done(dve.scalar_tensor_tensor(sv[:, 1, :], low, float(NT * R), sv[:, 0, :], ALU.mult, ALU.add))
            done(dve.tensor_tensor(idx_all[:, 1, 0:CH], sv[:, 1, :], low_s[:, 0:CH], ALU.add))
            dve.tensor_copy(low_s[:, 0:CH], low).then_inc(idx_ready, 1)

            def edges(half):
                dve.wait_ge(agg_set, 16 * (half + 1))
                per = AHEAD
                with dve.Fori(0, PAIRS // per) as i:
                    for at in range(per):
                        for e in range(2):
                            c = i * (2 * per) + (2 * at + e)
                            s6 = 2 * (at % AHEAD) + e
                            dve.wait_ge(agg_mm, c + (half * CH + 1))
                            dve.tensor_scalar(onehot[:, e, 0:TP], iota[:, 0:TP], low_s[:, bass.ds(c, 1)], None, ALU.is_equal)
                            dve.wait_ge(msg_hi_done, c + (half * CH + 1))
                            dve.scalar_tensor_tensor(msg_lo[:, e, :], gath[:, s6, :], w_slot[:, s6, :], f(msg_hi[:, e, :]),
                                                     ALU.mult, ALU.subtract).then_inc(msg_lo_done, 1)
                        for e in range(2):
                            c = i * (2 * per) + (2 * at + e)
                            v = dve.value_load(tile_i[0:1, bass.ds(c, 1)], min_val=0, max_val=NT - 1)
                            dve.wait_ge(agg_mm, c + (half * CH + 3))
                            dve.wait_ge(agg_added, c + (half * CH + 2))
                            acc = agg[0:TP, bass.ds(v, 1), :]
                            dve.tensor_tensor(acc, acc, ab[e][0:TP, :].unsqueeze(1), ALU.add).then_inc(agg_added, 1)

            edges(0)
            edges(1)

            dve.wait_ge(s_bc, 48)
            n_root = [NT]

            def rstd(mean_var):
                dve.tensor_scalar(sm[0:TP, 0:1], mean_var[:, 1:2], LN_EPS, None, ALU.add).then_inc(sd_ready, 1)
                n_root[0] += 1
                dve.wait_ge(sd_done, n_root[0])
                done(dve.reciprocal(mean_var[:, 1:2], sm[0:TP, 0:1]))

            def first_half(t):
                s = t % 2
                a, r, xx, z = (b[s][0:TP, :] for b in (A, Rr, Xx, Zz))
                dve.wait_ge(d_in[s], 64 * (t // 2 + 1))
                dve.tensor_tensor(a, a, r, ALU.add).then_inc(u_ready, 1)
                lo_half(dve, 2 * NT + 2 * t, t)
                dve.wait_ge(th_done, t + 1)
                done(dve.tensor_scalar(a, xx, mv[0:TP, t, 0:1], mv[0:TP, t, 1:2], ALU.subtract, ALU.mult))
                dve.tensor_tensor(r, r, a, ALU.subtract).then_inc(xl2_ready, 1)

            first_half(0)
            for t in range(NT):
                if t + 1 < NT:
                    first_half(t + 1)
                s = t % 2
                a, r, xx, z = (b[s][0:TP, :] for b in (A, Rr, Xx, Zz))
                dve.wait_ge(base_ready, t + 1)
                for j in range(NH):
                    dve.wait_ge(gate_ready, 2 * t + j + 1)
                    dve.tensor_tensor(z[:, j * H:(j + 1) * H], yb[j][0:TP, :], z[:, j * H:(j + 1) * H], ALU.add
                                      ).then_inc(gate_taken, 1)
                dve.wait_ge(gate_taken, 2 * t + 2)
                done(dve.tensor_tensor(z, z, r, ALU.mult))
                dve.tensor_tensor(z, z, xx, ALU.add).then_inc(y2_ready, 1)
                dve.wait_ge(y2_ready, t + 1)
                mvt = sm[0:TP, 2:4]
                row_stats(z, mvt, 0)
                rstd(mvt)
                done(dve.tensor_scalar(a, z, mvt[:, 0:1], mvt[:, 1:2], ALU.subtract, ALU.mult))
                row_stats(a, mvt, 0)
                rstd(mvt)
                dve.tensor_scalar(a, a, mvt[:, 0:1], mvt[:, 1:2], ALU.subtract, ALU.mult).then_inc(n_ready, 1)
                dve.wait_ge(xn_ready, t + 1)
                dve.tensor_reduce(amax[0:TP, t:t + 1], a, AX.X, ALU.max, apply_absolute_value=True).then_inc(xn_maxed, 1)
            dve.wait_ge(xn_maxed, NT)
            dve.tensor_reduce(gmx[0:TP, :], amax[0:TP, :], AX.X, ALU.max).then_inc(gm_in, 1)
            dve.wait_ge(gm_out, 1)
            done(dve.tensor_scalar(gms[0:TP, :], gms[0:TP, :], 1e-8, 1.0 / 127.0, ALU.max, ALU.mult))
            done(dve.reciprocal(qinv[0:TP, :], gms[0:TP, :]))
            done(dve.tensor_tensor(outscale[0:TP, :], gms[0:TP, :], alpha[0:TP, :], ALU.mult))
            for t in range(NT + 1):
                if t < NT:
                    s = t % 2
                    a = A[s][0:TP, :]
                    dve.wait_ge(e2_in[s], 32 * (t // 2 + 1))
                    done(dve.tensor_scalar(a, a, qinv[0:TP, :], 127.0, ALU.mult, ALU.min))
                    done(dve.tensor_scalar(a, a, -127.0, MAGIC, ALU.max, ALU.add))
                    if t >= 2:
                        dve.wait_ge(qt_ready, t - 1)
                    dve.tensor_scalar(Qb[s][0:TP, :], a, -MAGIC, None, ALU.add).then_inc(q_ready, 1)
                if t >= 1:
                    m = t - 1
                    z = Zz[m % 2][0:TP, :]
                    for j in range(NH):
                        dve.wait_ge(f_ready, 2 * m + j + 1)
                        zj = z[:, j * H:(j + 1) * H]
                        dve.scalar_tensor_tensor(zj, yb[j][0:TP, :], outscale[0:TP, :], zj, ALU.mult, ALU.add
                                                 ).then_inc(f_done, 1)

        @block.gpsimd
        def _(pool):
            pool.iota(iota[:, :], pattern=[[1, CH]], base=0, channel_multiplier=0,
                      allow_small_or_imprecise_dtypes=True).then_inc(s_const, 1)
            for n, m in enumerate((ident, ident_b, low_tri, ones_b)):
                pool.memset(m[:, :] if n < 2 else m, 1.0).then_inc(s_const, 1)
            pool.wait_ge(s_const, 5)
            pool.affine_select(out=ident[:, :], in_=ident[:, :], compare_op=ALU.is_equal, fill=0.0, base=0,
                               pattern=[[-1, P]], channel_multiplier=1)
            pool.affine_select(out=ident_b[:, :], in_=ident_b[:, :], compare_op=ALU.is_equal, fill=0.0, base=0,
                               pattern=[[-1, P]], channel_multiplier=1)
            pool.affine_select(out=low_tri, in_=low_tri, compare_op=ALU.is_gt, fill=0.0, base=0,
                               pattern=[[1, 128]], channel_multiplier=-1).then_inc(s_const, 1)
            pool.memset(idx_all[:, :, :], 0).then_inc(s_const, 1)
            pool.sem_inc(agg_mm, 2)

            def w_split_lo(done_hi, s, k):
                pool.wait_ge(w_hi_done, done_hi)
                pool.tensor_tensor(w_lo[:, s, k, :], w_stage[:, k % STG, :], f(w_hi[:, s, k, :]), ALU.subtract
                                   ).then_inc(w_lo_done, 1)

            for k in range(KT):
                w_split_lo(k + 1, 0, k)
            for n in range(2):
                pool.wait_ge(part_in, n + 1)
                pool.partition_all_reduce(psums[:, 0:2], both, P, bass.bass_isa.ReduceOp.add).then_inc(part_out, 1)

            def gather_pair(p, r3, half, prologue):
                pool.tensor_copy(idx_slot[:, r3, :, :], idx_all[:, :, bass.ds(p * 2, 2)] if not isinstance(p, int)
                                 else idx_all[:, :, 2 * p:2 * p + 2]).then_inc(icopy, 1)
                pool.wait_ge(icopy, p + (half * CHX // 2 + 1))
                pool.sem_inc(icopy_seen, 1)
                for e in range(2):
                    s6 = 2 * r3 + e
                    pool.indirect_dma_start(out=w_slot[:, s6, :], out_offset=None, in_=inv_dram,
                                            in_offset=bass.IndirectOffsetOnAxis(ap=idx_slot[:, r3, 1, e:e + 1], axis=0)
                                            ).then_inc(gw_landed[s6], 16)
                    pool.indirect_dma_start(out=gath[:, s6, :], out_offset=None, in_=y_dram[half],
                                            in_offset=bass.IndirectOffsetOnAxis(ap=idx_slot[:, r3, 0, e:e + 1], axis=0)
                                            ).then_inc(g_landed[s6], 16)

            def set_agg(half):
                pool.dma_start(agg[0:TP, :, :], bias[half * H:(half + 1) * H].unsqueeze(0).unsqueeze(0).to_broadcast([TP, NT, H])
                               ).then_inc(agg_set, 16)

            def save_agg(half):
                pool.wait_ge(agg_added, CH * (half + 1) + 2)
                pool.dma_start(agg_dram[:, half * H:(half + 1) * H].rearrange("(t p) c -> p t c", p=TP), agg[0:TP, :, :]
                               ).then_inc(agg_out, 16)
                pool.wait_ge(agg_out, 16 * (half + 1))

            def units(first, iters, pairs, half):
                with pool.Fori(0, iters) as i:
                    for s in range(2):
                        u = i * 2 + (first + s)
                        for m in range(NT):
                            if pairs is not None:
                                per, at0 = sum(pairs), sum(pairs[:s * NT + m])
                                for q in range(pairs[s * NT + m]):
                                    at = at0 + q
                                    p = i * per + (at + AHEAD)
                                    pool.wait_ge(msg_lo_done, i * (2 * per) + (2 * (at + 1) + half * CH))
                                    gather_pair(p, at % AHEAD, half, False)
                            if 1 <= m <= KT:
                                w_split_lo(u * KT + (KT + m), 1 - s, m - 1)

            units(*LOOPS[0])
            units(*LOOPS[1])
            pool.wait_ge(idx_ready, 1)
            pool.dma_start(inv_dram.rearrange("(p c) o -> p (c o)", p=P), big[:, 2048:2048 + NT * R]).then_inc(s_inv, 16)
            pool.wait_ge(s_inv, 16)
            pool.wait_ge(idx_ready, 2)
            set_agg(0)
            for half in range(NH):
                if half == 1:
                    save_agg(0)
                    set_agg(1)
                for q in range(2):
                    pool.wait_ge(y_stored[q], 16 * (half + 1) * R * NT // 2)
                for p in range(AHEAD):
                    if half == 1:
                        pool.wait_ge(msg_lo_done, CH)
                        for e in range(2):
                            pool.wait_ge(g_landed[2 * p + e], 16 * CHX // GS)
                            pool.wait_ge(gw_landed[2 * p + e], 16 * CHX // GS)
                    gather_pair(p, p, half, True)
                units(*LOOPS[2 + half])
            save_agg(1)
            for k in range(KT):
                w_split_lo(21 * KT + k + 1, 1, k)
            for q in range(GS):
                pool.wait_ge(g_landed[q], 32 * CHX // GS)
                pool.wait_ge(gw_landed[q], 32 * CHX // GS)
            pool.wait_ge(y_stored[0], 16 * 20 * NT // 2)
            pool.wait_ge(y_stored[1], 16 * 20 * NT // 2)
            for ap, dest in ((bgate, EV), (gamma, X0), (beta, X1)):
                pool.dma_start(dest[0:TP, :], ap.unsqueeze(0).to_broadcast([TP, D])).then_inc(s_bc, 16)
            pool.wait_ge(s_bc, 48)
            for t in range(NT + 1):
                if t < NT:
                    s = t % 2
                    pool.wait_ge(xl2_ready, t + 1)
                    pool.tensor_tensor(Xx[s][0:TP, :], Xx[s][0:TP, :], A[s][0:TP, :], ALU.add)
                    pool.tensor_tensor(Zz[s][0:TP, :], Zz[s][0:TP, :], EV[0:TP, :], ALU.add).then_inc(base_ready, 1)
                if t >= 1:
                    s = (t - 1) % 2
                    pool.wait_ge(n_ready, t)
                    pool.tensor_tensor(A[s][0:TP, :], A[s][0:TP, :], X0[0:TP, :], ALU.mult).then_inc(icopy, 1)
                    pool.wait_ge(icopy, CHX + t)
                    pool.tensor_tensor(A[s][0:TP, :], A[s][0:TP, :], X1[0:TP, :], ALU.add).then_inc(xn_ready, 1)
            pool.wait_ge(gm_in, 1)
            pool.partition_all_reduce(gms[0:TP, :], gmx[0:TP, :], TP, bass.bass_isa.ReduceOp.max).then_inc(gm_out, 1)


def kernel(**inputs):
    import numpy as np
    from concourse import bacc
    from concourse.bass_utils import run_bass_kernel_spmd

    a = {k: np.asarray(v) for k, v in inputs.items()}
    rel, root, wg = a["L0_gnn_weight"], a["L0_gnn_root"], a["L0_gnn_w_gate"]
    mats = [(rel[r], j) for j in range(NH) for r in range(R)]
    mats += [(m, j) for m in (root, wg[D:], wg[:D]) for j in range(NH)]
    wall = np.concatenate([m[:, j * H:(j + 1) * H] for m, j in mats], axis=0)
    arrays = {
        "x": a["x"], "src": a["src"], "dst": a["dst"], "edge_type": a["edge_type_8"], "weights": wall,
        "bias": a["L0_gnn_bias"], "b_gate": a["L0_gnn_b_gate"], "ffn_weight": a["L0_ffn_weight"],
        "ffn_gamma": a["L0_ffn_gamma"], "ffn_beta": a["L0_ffn_beta"],
    }
    arrays = {k: np.ascontiguousarray(v) for k, v in arrays.items()}
    nc = bacc.Bacc("TRN2", target_bir_lowering=False, num_devices=1)
    args = [nc.dram_tensor(f"in_{k}", v.shape, mybir.dt.from_np(v.dtype), kind="ExternalInput").ap()
            for k, v in arrays.items()]
    args.append(nc.dram_tensor("out_y", (N, D), F32, kind="ExternalOutput").ap())
    build(nc, *args)
    r = run_bass_kernel_spmd(nc, [{f"in_{k}": v for k, v in arrays.items()}], core_ids=[0])
    return r.results[0]["out_y"]
```

```python
import contextlib
from contextlib import ExitStack

import concourse.bass as bass
from concourse import mybir

F32, F32R = mybir.dt.float32, mybir.dt.float32r
F16, BF16, I32 = mybir.dt.float16, mybir.dt.bfloat16, mybir.dt.int32
ALU = mybir.AluOpType
ACT = mybir.ActivationFunctionType
AX = mybir.AxisListType

P = 128
N, D, R, E = 1250, 1024, 8, 20000
TP = 125
NT = N // TP
KT = D // P
H = 512
NH = D // H
EC = E // TP
PAIRS = 84
CH = 2 * PAIRS
AHEAD = 3
GS = 2 * AHEAD
CHX = CH + GS
STG = 4
NB = 5
LN_EPS = 1e-5
MAGIC = 1.5 * 2.0 ** 23
assert CH * P >= E + NT * (P - 1) - (P - 1) and EC % NB == 0


def build(nc, x, src, dst, etype, wall, bias, bgate, wffn, gamma, beta, out):
    ctx = ExitStack()
    with ctx:
        def sb(name, shape, dt):
            return ctx.enter_context(nc.sbuf_tensor(name, shape, dt))

        def sem(name):
            return ctx.enter_context(nc.semaphore(name))

        y_dram = [nc.dram_tensor(f"y_dram{j}", [R * N, H], F32, kind="Internal").ap() for j in range(NH)]
        rz_dram = nc.dram_tensor("rz_dram", [2 * NH * N, H], F32, kind="Internal").ap()
        agg_dram = nc.dram_tensor("agg_dram", [N, H], F32, kind="Internal").ap()
        inv_dram = nc.dram_tensor("inv_dram", [P * NT * R, 1], F32, kind="Internal").ap()
        tern_dram = nc.dram_tensor("tern_dram", [KT * P, D], BF16, kind="Internal").ap()
        y2_dram = nc.dram_tensor("y2_dram", [N, D], F32, kind="Internal").ap()
        xn_dram = nc.dram_tensor("xn_dram", [N, D], F32, kind="Internal").ap()

        xt_hi = sb("xt_hi", [P, KT, N], F32R)
        xt_lo = sb("xt_lo", [P, KT, N], F32R)
        w_hi = sb("w_hi", [P, 2, KT, H], F32R)
        w_lo = sb("w_lo", [P, 2, KT, H], F32R)
        w_stage = sb("w_stage", [P, STG, H], F32)
        agg = sb("agg", [P, NT, H], F32)
        gath = sb("gath", [P, GS, H], F32)
        msg_hi = sb("msg_hi", [P, 2, H], F32R)
        msg_lo = sb("msg_lo", [P, 2, H], F32R)
        onehot = sb("onehot", [P, 2, TP + 1], F32R)
        evict = sb("evict", [P, 2, H], F32)
        extra = sb("extra", [P, 2 * D], F32)
        idx_all = sb("idx_all", [P, 2, CHX], I32)
        low_s = sb("low_s", [P, CHX], F32)
        tile_i = sb("tile_i", [1, CHX], mybir.dt.int16)
        iota = sb("iota", [P, CH], F32)
        ident = sb("ident", [P, P], F32)
        ident_b = sb("ident_b", [P, P], BF16)
        idx_slot = sb("idx_slot", [P, AHEAD, 2, 2], I32)
        w_slot = sb("w_slot", [P, GS, 1], F32)
        mv = sb("mv", [P, NT, 2], F32)
        stats = sb("stats", [P, 2, 6], F32)
        sm = sb("sm", [P, 64], F32)
        amax = sb("amax", [P, NT], F32)

        def bank(name):
            return ctx.enter_context(nc.psum_tensor(name, [P, H], F32))
        yb = [bank("yb0"), bank("yb1")]
        ab = [bank("ab0"), bank("ab1")]
        tb = [bank("tb0"), bank("tb1")]
        perm_b, cnt_b = bank("perm_b"), bank("cnt_b")
        fb = yb + ab

        big = agg[:, :, :].rearrange("p t c -> p (t c)")
        gbig = gath[:, :, :].rearrange("p s c -> p (s c)")
        T = [big[:, i * D:(i + 1) * D] for i in range(5)]
        G = [gbig[:, i * D:(i + 1) * D] for i in range(3)]
        EV = evict[:, :, :].rearrange("p s c -> p (s c)")
        X0, X1 = extra[:, 0:D], extra[:, D:2 * D]

        s_const = sem("s_const")
        s_x = [sem(f"s_x{t}") for t in range(NT)]
        s_dve = sem("s_dve")
        xl_ready = sem("xl_ready")
        tr_ready = sem("tr_ready")
        tr_hi = sem("tr_hi")
        tr_lo = sem("tr_lo")
        sd_ready = sem("sd_ready")
        sd_done = sem("sd_done")
        s_edges = sem("s_edges")
        oh_tile = sem("oh_tile")
        rank_ready = sem("rank_ready")
        rank_used = sem("rank_used")
        s_wf = [sem("s_wf0"), sem("s_wf1")]
        wf_used = sem("wf_used")
        tern_ready = sem("tern_ready")
        tern_t = sem("tern_t")
        tern_c = sem("tern_c")
        tern_st = [sem("tern_st0"), sem("tern_st1")]
        part_in = sem("part_in")
        part_out = sem("part_out")
        w_landed = [sem(f"w_landed{i}") for i in range(STG)]
        w_hi_done = sem("w_hi_done")
        w_lo_done = sem("w_lo_done")
        y_ready = sem("y_ready")
        y_free = sem("y_free")
        y_stored = [sem("y_stored0"), sem("y_stored1")]
        oh_ready = sem("oh_ready")
        oh_used = sem("oh_used")
        eq_ready = sem("eq_ready")
        idx_ready = sem("idx_ready")
        s_inv = sem("s_inv")
        scratch_free = sem("scratch_free")
        agg_set = sem("agg_set")
        agg_out = sem("agg_out")
        icopy = sem("icopy")
        icopy_seen = sem("icopy_seen")
        g_landed = [sem(f"g_landed{i}") for i in range(GS)]
        gw_landed = [sem(f"gw_landed{i}") for i in range(GS)]
        msg_hi_done = sem("msg_hi_done")
        msg_lo_done = sem("msg_lo_done")
        agg_mm = sem("agg_mm")
        agg_added = sem("agg_added")
        w_kept = sem("w_kept")
        u_summed = [[sem("u_summed_left")] * NT, [sem(f"u_summed{t}") for t in range(NT)]]
        a_in = [sem("a_in0"), sem("a_in1")]
        x_in = [sem("x_in0"), sem("x_in1")]
        z_in = [sem("z_in0"), sem("z_in1")]
        y2_out = [sem("y2_out0"), sem("y2_out1")]
        xn_out = [sem("xn_out0"), sem("xn_out1")]
        s_nm = sem("s_nm")
        th_done = sem("th_done")
        xl2_ready = sem("xl2_ready")
        base_ready = sem("base_ready")
        s_bc = sem("s_bc")
        gate_ready = sem("gate_ready")
        gate_taken = sem("gate_taken")
        y2_ready = sem("y2_ready")
        n_ready = sem("n_ready")
        xn_ready = sem("xn_ready")
        xn_maxed = sem("xn_maxed")
        gm_in = sem("gm_in")
        gm_out = sem("gm_out")
        s_tern = sem("s_tern")
        xe_in = [sem(f"xe_in{q}") for q in range(3)]
        ze_in = [sem(f"ze_in{q}") for q in range(3)]
        q_ready = sem("q_ready")
        qt_ready = sem("qt_ready")
        qt_done = sem("qt_done")
        f_ready = sem("f_ready")
        f_done = sem("f_done")
        o_out = [sem(f"o_out{q}") for q in range(3)]

        ex = [extra[0:TP, i * EC:(i + 1) * EC] for i in range(12)]
        srcf, dstf, typf, tile_a, tile_b, lowf, bfld, k80, pcf, plf = ex[2:12]
        ei = [ex[i].bitcast(I32) for i in (0, 1)]
        C16 = NT * EC
        cumT, cumI = big[:, 0:C16], big[:, C16:2 * C16]
        rankV = big[0:TP, 2 * C16:3 * C16]
        g16 = gbig[0:TP, :].bitcast(BF16)
        oh_t, low_tri, ones_b = g16[:, 0:C16], g16[:, C16:C16 + 128], g16[:, C16 + 128:C16 + 256]
        G2b = T[2]
        tern_out = [T[3].bitcast(BF16)[:, q * D:(q + 1) * D] for q in range(2)]
        big16 = big[0:TP, :].bitcast(F16)
        w_all = idx_all[:, 1, :].bitcast(F32)
        OHW = NB * (P + 2 * CH + CH + TP + 3 + NT * R)

        def batch_slot(s):
            at, res = s * OHW, []
            for w in (P, 2 * CH, CH, TP + 3, NT * R):
                res.append(big16[:, at:at + NB * w].rearrange("p (c w) -> p c w", c=NB))
                at += NB * w
            return res
        batches = [batch_slot(0), batch_slot(1)]

        tern_v = [gbig.bitcast(BF16)[:, i * D:(i + 1) * D] for i in range(6)] + \
                 [T[4].bitcast(BF16)[:, i * D:(i + 1) * D] for i in range(2)]
        tern_w = big[:, D:5 * D].bitcast(BF16).rearrange("p (o k c) -> p o k c", o=KT, k=KT)

        WS = w_stage[:, :, :].rearrange("p s c -> p (s c)")
        A = [G[0], G[1]]
        Xx = [G[2], T[0]]
        Rr = [T[1], T[2]]
        Zz = [T[3], T[4]]
        Xn = [WS[:, 0:D], WS[:, D:2 * D]]
        Xe = [G[0], G[1], G[2]]
        Ze = [T[0], WS[:, 0:D], WS[:, D:2 * D]]
        exb, evb = extra[:, :].bitcast(BF16), EV.bitcast(BF16)
        Qb = [exb[:, 0:D], exb[:, D:2 * D], exb[:, 2 * D:3 * D]]
        qT = [q[:, 0:KT * TP].rearrange("p (k n) -> p k n", k=KT) for q in (exb[:, 3 * D:4 * D], evb[:, 0:D])]
        XA = T + G + [X0, X1]

        cntt, capt, base, delta_t, cap_i, tmp10 = (sm[:, 10 * i:10 * i + 10] for i in range(6))
        smc = lambda i: sm[:, 60 + i:61 + i]
        nmean = amax
        asum = sb("asum", [P, 2 * KT + 7], F32)
        thr, nthr, alpha = asum[:, 2 * KT:2 * KT + 1], asum[:, 2 * KT + 1:2 * KT + 2], asum[:, 2 * KT + 2:2 * KT + 3]
        tot_s, tot_n = asum[:, 2 * KT + 3:2 * KT + 4], asum[:, 2 * KT + 4:2 * KT + 5]
        both = asum[:, 2 * KT + 3:2 * KT + 5]
        psums = asum[:, 2 * KT + 5:2 * KT + 7]
        gmx, qinv = smc(0), smc(1)
        outscale, gms = smc(2), smc(3)

        rows = lambda ap, t: ap[t * TP:(t + 1) * TP, :]
        rz_v = rz_dram.rearrange("(u n) c -> n u c", u=2 * NH)
        f = lambda ap: ap.bitcast(F32)

        pairs_b1 = [0] + [2 if m in (7, 14) else 1 for m in range(1, 2 * NT)]
        pairs_c1 = [0] * 3 + [3 if m % 2 == 0 and m < 18 else 2 for m in range(3, 2 * NT)]
        pairs_c2 = [3 if m in (5, 10, 15) else 2 for m in range(2 * NT)]
        assert sum(pairs_b1) == PAIRS // 4 and sum(pairs_c1) + sum(pairs_c2) == PAIRS
        LOOPS = (
            (0, 1, None, None),
            (2, 1, None, None),
            (4, 2, None, None),
            (8, 4, pairs_b1, 0),
            (16, 1, pairs_c1, 1), (18, 1, pairs_c2, 1))

        def loop(eng, iters):
            return eng.Fori(0, iters) if iters > 1 else contextlib.nullcontext(0)

        def sorts(n, s, m):
            return n == 2 and s * NT + m < EC // NB // 2

        block = ctx.enter_context(nc.Block())

        def with_pairs(n, s, m):
            pairs = LOOPS[n][2]
            if pairs is None:
                return []
            at = sum(pairs[:s * NT + m])
            return range(at, at + pairs[s * NT + m])

        def before(n):
            return sum(lp[1] * sum(lp[2]) for lp in LOOPS[:n] if lp[2] and lp[3] == LOOPS[n][3])

        def lo_half(dve, n0, t):
            for h in range(2):
                dve.wait_ge(tr_hi, n0 + h + 1)
                dst3 = (xt_lo[:, 4 * h:4 * h + 4, t * TP:(t + 1) * TP])
                hi3 = f(xt_hi[:, 4 * h:4 * h + 4, t * TP:(t + 1) * TP])
                dve.tensor_tensor(dst3, tb[h][:, 0:4 * TP].rearrange("p (k n) -> p k n", k=4), hi3,
                                  ALU.subtract).then_inc(tr_lo, 1)

        @block.sync
        def _(sp):
            def load_w(g, k):
                sp.dma_start(w_stage[:, k % STG, :], wall[g * P:(g + 1) * P, :]).then_inc(w_landed[k % STG], 16)

            for t in range(NT):
                sp.dma_start(XA[t][0:TP, :], rows(x, t)).then_inc(s_x[t], 16)
                if t % 2 == 1 and t // 2 < STG:
                    load_w(t // 2, t // 2)
            for k in range(STG, KT):
                sp.wait_ge(w_lo_done, k - STG + 1)
                load_w(k, k)

            for n, (first, iters, _, half) in enumerate(LOOPS):
                table, t0 = ((y_dram[0], 0), (y_dram[1], 8), (rz_dram, 16))[0 if first < 8 else 1 if first < 16 else 2]
                with loop(sp, iters) as i:
                    for s in range(2):
                        u = i * 2 + (first + s)
                        for m in range(NT):
                            if m < KT:
                                sp.wait_ge(w_lo_done, u * KT + (KT + m - STG + 1))
                                sp.dma_start(w_stage[:, m % STG, :], wall[bass.ds(u * (KT * P) + (KT + m) * P, P), :]
                                             ).then_inc(w_landed[m % STG], 16)
                            if n == 0 and s == 0 and m == 5:
                                sp.wait_ge(tr_lo, 2 * NT)
                                for a, t in ((src, ei[0]), (dst, ei[1]), (etype, ex[11].bitcast(I32))):
                                    sp.dma_start(t, a.rearrange("(p c) -> p c", p=TP)).then_inc(s_edges, 16)
                            sp.wait_ge(y_free, u * NT + (m + 3))
                            sp.dma_start(table[bass.ds(i * (2 * N) + ((first - t0 + s) * N + m * TP), TP), :],
                                         evict[0:TP, m % 2, :]).then_inc(y_stored[m % 2], 16)
                            if n == 1 and s == 1 and m < KT:
                                sp.wait_ge(tern_c, m + 1)
                                sp.dma_start(tern_dram[m * P:(m + 1) * P, :], tern_out[m % 2]
                                             ).then_inc(tern_st[m % 2], 16)
            for k in range(KT):
                sp.wait_ge(w_lo_done, 21 * KT + k - STG + 1)
                load_w(21 * KT + k, k)
            for t in range(NT + 2):
                s = t % 2
                if t < NT:
                    for q in range(NH):
                        sp.wait_ge(u_summed[q][t], 16)
                    if t >= 2:
                        sp.wait_ge(base_ready, t - 1)
                    else:
                        for q in range(GS):
                            sp.wait_ge(g_landed[q], 16 * (CHX + CH) // GS)
                    sp.dma_start(A[s][0:TP, :].rearrange("p (u c) -> p u c", u=2), rz_v[t * TP:(t + 1) * TP, 0:2, :]
                                 ).then_inc(a_in[s], 16)
                    if t == 0:
                        for q in range(NT):
                            sp.wait_ge(u_summed[1][q], 16)
                    if t >= 2:
                        sp.wait_ge(y2_ready, t - 1)
                    sp.dma_start(Xx[s][0:TP, :], rows(x, t)).then_inc(x_in[s], 16)
                if t >= 2:
                    sp.wait_ge(y2_ready, t - 1)
                    sp.dma_start(rows(y2_dram, t - 2), Zz[s][0:TP, :]).then_inc(y2_out[s], 16)
                    if t < NT:
                        sp.wait_ge(y2_out[s], 16 * (t // 2))
                        sp.wait_ge(n_ready, t - 1)
                if t < NT:
                    sp.dma_start(Zz[s][0:TP, :].rearrange("p (u c) -> p u c", u=2), rz_v[t * TP:(t + 1) * TP, 2:4, :]
                                 ).then_inc(z_in[s], 16)
                if t >= 2:
                    sp.wait_ge(xn_ready, t - 1)
                    sp.dma_start(rows(xn_dram, t - 2), Xn[s][0:TP, :]).then_inc(xn_out[s], 16)
            for q in range(2):
                sp.wait_ge(y2_out[q], 16 * NT // 2)
                sp.wait_ge(xn_out[q], 16 * NT // 2)
            sp.wait_ge(xn_maxed, NT)

            def load_e(t):
                if t >= 3:
                    sp.wait_ge(q_ready, t - 2)
                sp.dma_start(Xe[t % 3][0:TP, :], rows(xn_dram, t)).then_inc(xe_in[t % 3], 16)
                if t >= 3:
                    sp.wait_ge(o_out[t % 3], 16 * (t // 3))
                sp.dma_start(Ze[t % 3][0:TP, :], rows(y2_dram, t)).then_inc(ze_in[t % 3], 16)
            load_e(0)
            load_e(1)
            sp.dma_start(tern_w.rearrange("p o k c -> p o (k c)"), tern_dram.rearrange("(o p) c -> p o c", p=P)).then_inc(s_tern, 16)
            load_e(2)
            for t in range(NT):
                sp.wait_ge(f_done, 2 * (t + 1))
                sp.dma_start(rows(out, t), Ze[t % 3][0:TP, :]).then_inc(o_out[t % 3], 16)
                if t + 3 < NT:
                    load_e(t + 3)
            for q in range(3):
                sp.wait_ge(o_out[q], 16 * ((NT + 2 - q) // 3))

        @block.tensor
        def _(pe):
            def transpose_tile(src_tile, n0):
                for h in range(2):
                    if n0 + h >= 2:
                        pe.wait_ge(tr_lo, n0 + h - 1)
                    for q in range(4):
                        ins = pe.transpose(tb[h][:, q * TP:(q + 1) * TP],
                                           src_tile[0:TP, (4 * h + q) * P:(4 * h + q + 1) * P], ident[0:TP, 0:TP])
                    ins.then_inc(tr_ready, 1)

            def ranks():
                w2 = 2 * EC
                pe.wait_ge(s_const, 7)
                pe.wait_ge(oh_tile, 1)
                for q in range(NT // 2):
                    for n, tri, m in ((2 * q, ones_b, P), (2 * q + 1, low_tri, TP)):
                        if n >= 2:
                            pe.wait_ge(rank_used, n - 1)
                        pe.matmul(ab[n % 2][0:m, 0:w2], tri[:, 0:m], oh_t[:, q * w2:(q + 1) * w2], start=True, stop=True
                                  ).then_inc(rank_ready, 1)

            def chunk(c, e):
                pe.wait_ge(msg_lo_done, c + 1)
                pe.wait_ge(agg_added, c + 1)
                pe.matmul(ab[e][0:TP, :], onehot[:, e, 0:TP], msg_hi[:, e, :], start=True, stop=False)
                pe.matmul(ab[e][0:TP, :], onehot[:, e, 0:TP], msg_lo[:, e, :], start=False, stop=True
                          ).then_inc(agg_mm, 1)

            def sort_batch(b, s):
                ohl, rhs, _, ohlow, oh80 = batches[s]
                pe.wait_ge(oh_ready, b + 1)
                for c in range(NB):
                    end = c == NB - 1
                    pe.matmul(perm_b[:, 0:2 * CH], ohl[:, c, :], rhs[:, c, :], start=False, stop=end, skip_group_check=True)
                    ins = pe.matmul(cnt_b[0:TP, 0:NT * R], ohlow[:, c, 0:TP], oh80[:, c, :], start=False, stop=end,
                                    skip_group_check=True)
                ins.then_inc(oh_used, 1)

            def products(bank_j, s, k, m):
                xh, xl = xt_hi[:, k, m * TP:(m + 1) * TP], xt_lo[:, k, m * TP:(m + 1) * TP]
                o = bank_j[0:TP, :]
                pe.matmul(o, xh, w_hi[:, s, k, :], start=k == 0, stop=False)
                pe.matmul(o, xh, w_lo[:, s, k, :], start=False, stop=False)
                return pe.matmul(o, xl, w_hi[:, s, k, :], start=False, stop=k == KT - 1)

            pe.wait_ge(s_const, 5)
            for n, (first, iters, pairs, half) in enumerate(LOOPS):
                with loop(pe, iters) as i:
                    for s in range(2):
                        for m in range(NT):
                            u = i * 2 + (first + s)
                            if n == 0 and s == 0:
                                for t in (2 * m, 2 * m + 1) if m < NT // 2 else ():
                                    pe.wait_ge(xl_ready, t + 1)
                                    transpose_tile(XA[t], 2 * t)
                                pe.wait_ge(tr_lo, 2 * (m + 1))
                            todo = [(i * (2 * sum(pairs)) + (2 * (before(n) + p) + e + half * CH), e)
                                    for p in with_pairs(n, s, m) for e in range(2)]
                            pe.wait_ge(y_free, u * NT + (m + 1))
                            gaps = {}
                            for q in range(len(todo)):
                                gaps.setdefault(KT - 1 - (len(todo) - 1 - q) * (1 if len(todo) > 2 else 2), []).append(todo[q])
                            for k in range(KT):
                                if m == 0:
                                    pe.wait_ge(w_lo_done, u * KT + (k + 1))
                                ins = products(yb[m % 2], s, k, m)
                                if k == KT - 1:
                                    ins.then_inc(y_ready, 1)
                                for c, e in gaps.get(k, []):
                                    chunk(c, e)
                            if n == 0 and (s, m) == (0, NT - 1):
                                ranks()
                            if n == 1 and s == 1 and m < KT:
                                pe.wait_ge(tern_ready, m + 1)
                                if m >= 2:
                                    pe.wait_ge(tern_c, m - 1)
                                tbb = tb[m % 2][:, :].bitcast(BF16)
                                for k in range(KT):
                                    ins = pe.transpose(tbb[:, k * P:(k + 1) * P], tern_v[m][:, k * P:(k + 1) * P], ident_b[:, :])
                                ins.then_inc(tern_t, 1)
                            if n == 1 and (s, m) == (1, NT - 1):
                                z = idx_all[:, :, :].rearrange("p a c -> p (a c)").bitcast(F16)
                                pe.matmul(perm_b[:, 0:2 * CH], z[:, 0:P], z[:, 0:2 * CH], start=True, stop=True)
                                pe.matmul(cnt_b[0:TP, 0:NT * R], z[:, 0:TP], z[:, 0:NT * R], start=True, stop=True)
                            if sorts(n, s, m):
                                sort_batch(i * (EC // NB // 2) + (s * NT + m), m % 2)

            for t in range(2):
                pe.wait_ge(a_in[t], 16)
                transpose_tile(A[t], 2 * NT + 2 * t)
            pe.wait_ge(w_lo_done, 22 * KT)
            for t in range(NT):
                pe.wait_ge(tr_lo, 2 * NT + 2 * (t + 1))
                for j in range(NH):
                    if t >= 1:
                        pe.wait_ge(gate_taken, 2 * (t - 1) + j + 1)
                    else:
                        pe.wait_ge(y_free, 20 * NT + 2)
                    for k in range(KT):
                        ins = products(yb[j], j, k, t)
                    ins.then_inc(gate_ready, 1)
                if t + 2 < NT:
                    pe.wait_ge(a_in[t % 2], 16 * (t // 2 + 2))
                    transpose_tile(A[t % 2], 2 * NT + 2 * (t + 2))

            def transpose_q(t):
                pe.wait_ge(q_ready, t + 1)
                if t >= 2:
                    pe.wait_ge(qt_done, t - 1)
                else:
                    pe.wait_ge(tr_lo, 4 * NT)
                tbb = tb[t % 2][:, :].bitcast(BF16)
                for k in range(KT):
                    ins = pe.transpose(tbb[:, k * P:k * P + TP], Qb[t % 3][0:TP, k * P:(k + 1) * P], ident_b[0:TP, 0:TP])
                ins.then_inc(qt_ready, 1)
            transpose_q(0)
            transpose_q(1)
            pe.wait_ge(s_tern, 16)
            for t in range(NT):
                pe.wait_ge(qt_done, t + 1)
                for j in range(NH):
                    n4 = 2 * (t % 2) + j
                    if t >= 2:
                        pe.wait_ge(f_done, 2 * (t - 2) + j + 1)
                    for k in range(KT):
                        ins = pe.matmul(fb[n4][0:TP, :], qT[t % 2][:, k, :], tern_w[:, 4 * j:4 * j + 4, k, :],
                                        start=k == 0, stop=k == KT - 1)
                    ins.then_inc(f_ready, 1)
                if t + 2 < NT:
                    transpose_q(t + 2)

        @block.scalar
        def _(act):
            def tr_half(n, t, h):
                act.wait_ge(tr_ready, n + 1)
                act.activation(xt_hi[:, 4 * h:4 * h + 4, t * TP:(t + 1) * TP],
                               tb[h][:, 0:4 * TP].rearrange("p (k n) -> p k n", k=4), ACT.Copy).then_inc(tr_hi, 1)

            def w_split_hi(landed, s, k):
                act.wait_ge(w_landed[k % STG], landed)
                act.activation(w_hi[:, s, k, :], w_stage[:, k % STG, :], ACT.Copy).then_inc(w_hi_done, 1)

            act.sem_inc(y_free, 2)
            for k in range(KT // 2):
                w_split_hi(16, 0, k)
            act.wait_ge(sd_ready, 1)
            act.activation(mv[0:TP, :, 1], mv[0:TP, :, 1], ACT.Sqrt).then_inc(sd_done, 1)
            for k in range(KT // 2, KT):
                w_split_hi(32, 0, k)

            for n, (first, iters, pairs, half) in enumerate(LOOPS):
                with loop(act, iters) as i:
                    for s in range(2):
                        u = i * 2 + (first + s)
                        for m in range(NT):
                            if n == 0 and s == 0 and m < NT // 2:
                                for t in (2 * m, 2 * m + 1):
                                    for h in range(2):
                                        tr_half(2 * t + h, t, h)
                            if 1 <= m <= KT:
                                k = m - 1
                                if k == 0 and first + s > 0:
                                    act.wait_ge(y_ready, u * NT)
                                w_split_hi(u * 32 + 16 * (2 + k // STG + 1), 1 - s, k)
                            for p in with_pairs(n, s, m):
                                q = before(n) + p
                                for e in range(2):
                                    s6 = 2 * (q % AHEAD) + e
                                    landed = i * (16 * sum(pairs) // AHEAD) + 16 * (q // AHEAD + 1)
                                    act.wait_ge(g_landed[s6], landed + 16 * half * CHX // GS)
                                    if half == 0:
                                        act.wait_ge(gw_landed[s6], landed)
                                        scale = w_slot[:, s6, :]
                                    else:
                                        scale = w_all[:, bass.ds(i * (2 * sum(pairs)) + (2 * q + e), 1)]
                                    act.wait_ge(agg_mm, i * (2 * sum(pairs)) + (2 * q + e + half * CH + 1))
                                    act.activation(msg_hi[:, e, :], gath[:, s6, :], ACT.Copy, scale=scale).then_inc(msg_hi_done, 1)
                            act.wait_ge(y_ready, u * NT + (m + 1))
                            if n > 0 or s > 0 or m > 1:
                                act.wait_ge(y_stored[m % 2], u * (16 * NT // 2) + 16 * (m // 2))
                            act.activation(evict[0:TP, m % 2, :], yb[m % 2][0:TP, :], ACT.Copy).then_inc(y_free, 1)
                            if n == 1 and s == 1 and m < KT:
                                act.wait_ge(tern_t, m + 1)
                                if m >= 2:
                                    act.wait_ge(tern_st[m % 2], 16 * (m // 2))
                                act.activation(tern_out[m % 2], tb[m % 2][:, :].bitcast(BF16), ACT.Copy
                                               ).then_inc(tern_c, 1)
            act.wait_ge(y_ready, 20 * NT)
            for k in range(KT):
                w_split_hi(16 * (21 * 2 + k // STG + 1), 1, k)

            def tanh(t):
                s = t % 2
                if t >= 2:
                    act.wait_ge(y2_ready, t - 1)
                else:
                    for q in range(NT):
                        act.wait_ge(u_summed[1][q], 16)
                act.activation(Rr[s][0:TP, :], A[s][0:TP, :], ACT.Tanh).then_inc(th_done, 1)
                act.wait_ge(th_done, t + 1)
                act.wait_ge(x_in[s], 16 * (t // 2 + 1))
                act.wait_ge(s_nm, 1)
                act.activation(A[s][0:TP, :], Xx[s][0:TP, :], ACT.Identity, bias=nmean[0:TP, t:t + 1],
                               scale=mv[0:TP, t, 1:2]).then_inc(xl2_ready, 1)
            for t in range(NT):
                if t < 2:
                    for h in range(2):
                        tr_half(2 * NT + 2 * t + h, t, h)
                    tanh(t)
            for t in range(NT):
                if t + 2 < NT:
                    for h in range(2):
                        tr_half(2 * NT + 2 * (t + 2) + h, t + 2, h)
                    tanh(t + 2)
                act.wait_ge(sd_ready, t + 2)
                act.activation(sm[0:TP, 0:1], sm[0:TP, 0:1], ACT.Sqrt).then_inc(sd_done, 1)
            for t in range(NT):
                act.wait_ge(qt_ready, t + 1)
                if t >= 2:
                    act.wait_ge(f_ready, 2 * (t - 1))
                act.activation(qT[t % 2], tb[t % 2][:, :].bitcast(BF16).rearrange("p (k n) -> p k n", k=KT)[:, :, 0:TP],
                               ACT.Copy).then_inc(qt_done, 1)

        @block.vector
        def _(dve):
            steps = [0]

            def done(ins):
                steps[0] += 1
                ins.then_inc(s_dve, 1)
                dve.wait_ge(s_dve, steps[0])

            dve.sem_inc(agg_added, 2)

            def row_stats(tile, mean_var, wait=True):
                for h in range(2):
                    done(dve.bn_stats(stats[0:TP, h, :], tile[:, h * H:(h + 1) * H]))
                done(dve.bn_aggr(mean_var, stats[0:TP, 0:2, :].rearrange("p a b -> p (a b)")))

            for t in range(NT):
                dve.wait_ge(s_x[t], 16)
                row_stats(XA[t][0:TP, :], mv[0:TP, t, :])
            dve.tensor_scalar(mv[0:TP, :, 1], mv[0:TP, :, 1], LN_EPS, None, ALU.add).then_inc(sd_ready, 1)
            dve.wait_ge(sd_done, 1)
            done(dve.reciprocal(mv[0:TP, :, 1], mv[0:TP, :, 1]))

            def normalise(t):
                dve.tensor_scalar(XA[t][0:TP, :], XA[t][0:TP, :], mv[0:TP, t, 0:1], mv[0:TP, t, 1:2], ALU.subtract, ALU.mult
                                  ).then_inc(xl_ready, 1)
            for t in range(2):
                normalise(t)
            for t in range(NT):
                if t + 2 < NT:
                    normalise(t + 2)
                lo_half(dve, 2 * t, t)

            dve.wait_ge(s_edges, 48)
            done(dve.tensor_copy(srcf, ei[0]))
            done(dve.tensor_copy(dstf, ei[1]))
            done(dve.tensor_scalar(tile_a, dstf, float(TP), None, ALU.is_ge))
            cur, nxt = tile_a, tile_b
            for t in range(2, NT):
                done(dve.scalar_tensor_tensor(nxt, dstf, float(t * TP), cur, ALU.is_ge, ALU.add))
                cur, nxt = nxt, cur
            tl = cur
            done(dve.scalar_tensor_tensor(lowf, tl, -float(TP), dstf, ALU.mult, ALU.add))
            for t in range(NT):
                ins = dve.tensor_scalar(oh_t[:, t * EC:(t + 1) * EC], tl, float(t), None, ALU.is_equal)
            ins.then_inc(oh_tile, 1)
            done(dve.tensor_copy(typf, ex[11].bitcast(I32)))
            done(dve.scalar_tensor_tensor(k80, tl, float(R), typf, ALU.mult, ALU.add))
            done(dve.scalar_tensor_tensor(bfld, typf, float(P), lowf, ALU.mult, ALU.add))
            done(dve.tensor_scalar(bfld, bfld, 1.0, None, ALU.add))
            for o in range(KT):
                dve.wait_ge(s_wf[o % 2], 16 * (o // 2 + 1))
                dve.tensor_reduce(asum[:, o:o + 1], T[o % 2], AX.X, ALU.add, apply_absolute_value=True).then_inc(wf_used, 1)
            dve.wait_ge(wf_used, KT)
            done(dve.tensor_reduce(tot_s, asum[:, 0:KT], AX.X, ALU.add))
            dve.memset(tot_n, 0.0).then_inc(part_in, 1)
            w2 = 2 * EC
            for q in range(NT // 2):
                for n, dest, m in ((2 * q, cumT, P), (2 * q + 1, rankV, TP)):
                    dve.wait_ge(rank_ready, n + 1)
                    dve.tensor_copy(dest[:, q * w2:(q + 1) * w2], ab[n % 2][0:m, 0:w2]).then_inc(rank_used, 1)
            dve.wait_ge(rank_used, NT)
            done(dve.tensor_tensor(rankV, rankV, cumT[0:TP, :], ALU.subtract))
            done(dve.memset(cumI, 0.0))
            done(dve.tensor_tensor_scan(cumI, cumI, cumT, 0.0, ALU.add, ALU.add))
            done(dve.tensor_tensor(rankV, rankV, cumI[0:TP, :], ALU.add))
            ends = cumI.rearrange("p (t c) -> p t c", t=NT)[:, :, EC - 1]
            done(dve.tensor_copy(tmp10, ends))
            done(dve.tensor_copy(cntt[:, 0:1], tmp10[:, 0:1]))
            done(dve.tensor_tensor(cntt[:, 1:NT], tmp10[:, 1:NT], tmp10[:, 0:NT - 1], ALU.subtract))
            done(dve.tensor_scalar(cap_i.bitcast(I32), cntt, float(P - 1), None, ALU.add))
            done(dve.tensor_scalar(cap_i.bitcast(I32), cap_i.bitcast(I32), -P, None, ALU.bitwise_and))
            done(dve.tensor_copy(capt, cap_i.bitcast(I32)))
            done(dve.memset(base, 0.0))
            done(dve.tensor_tensor_scan(base, base, capt, 0.0, ALU.add, ALU.add))
            done(dve.tensor_tensor(base, base, capt, ALU.subtract))
            done(dve.tensor_tensor(delta_t, base, tmp10, ALU.subtract))
            done(dve.tensor_tensor(delta_t, delta_t, cntt, ALU.add))
            v3 = rankV.rearrange("p (t c) -> p t c", t=NT)
            o3 = oh_t.rearrange("p (t c) -> p t c", t=NT)
            done(dve.tensor_tensor(v3, v3, delta_t[0:TP, :].unsqueeze(2).to_broadcast([TP, NT, EC]), ALU.add))
            done(dve.tensor_tensor(rankV, rankV, oh_t, ALU.mult))
            done(dve.tensor_reduce(pcf, rankV.rearrange("p (t c) -> p c t", t=NT), AX.X, ALU.add))
            pos_i, lane_i = tile_a.bitcast(I32), tile_b.bitcast(I32)
            done(dve.tensor_copy(pos_i, pcf))
            done(dve.tensor_scalar(lane_i, pos_i, P - 1, None, ALU.bitwise_and))
            done(dve.tensor_copy(plf, lane_i))
            done(dve.tensor_scalar(lane_i, pos_i, 7, None, ALU.arith_shift_right))
            done(dve.tensor_copy(pcf, lane_i))
            ca, cb = cumT[:, 0:CHX], cumT[:, CHX:2 * CHX]
            i128 = cumT[:, 2 * CHX:2 * CHX + CH]
            done(dve.tensor_scalar(i128, iota[:, :], float(P), None, ALU.mult))
            done(dve.memset(ca, float(NT - 1)))
            done(dve.memset(cb, float(NT - 1)))
            done(dve.tensor_scalar(ca[:, 0:CH], i128, base[:, 1:2], None, ALU.is_ge))
            for t in range(2, NT):
                done(dve.scalar_tensor_tensor(cb[:, 0:CH], i128, base[:, t:t + 1], ca[:, 0:CH], ALU.is_ge, ALU.add))
                ca, cb = cb, ca
            done(dve.tensor_copy(tile_i[0:1, :], ca[0:1, :]))
            dve.tensor_scalar(low_s[:, :], ca, float(R), None, ALU.mult).then_inc(scratch_free, 1)

            dve.wait_ge(part_out, 1)
            done(dve.tensor_scalar(thr, psums[:, 0:1], 1.0 / (D * D), None, ALU.mult))
            done(dve.tensor_scalar(thr, thr, 0.7, None, ALU.mult))
            done(dve.tensor_scalar(nthr, thr, -1.0, None, ALU.mult))
            for o in range(KT):
                dve.wait_ge(s_wf[o % 2], 16 * (KT // 2 + o // 2 + 1))
                w = T[o % 2]
                done(dve.tensor_scalar(G2b, w, nthr, None, ALU.is_lt))
                dve.scalar_tensor_tensor(tern_v[o], w, thr, G2b, ALU.is_gt, ALU.subtract).then_inc(tern_ready, 1)
                dve.wait_ge(tern_ready, o + 1)
                done(dve.scalar_tensor_tensor(G2b, w, 1.0, tern_v[o], ALU.mult, ALU.mult, accum_out=asum[:, o:o + 1]))
                dve.scalar_tensor_tensor(G2b, tern_v[o], 1.0, tern_v[o], ALU.mult, ALU.mult,
                                         accum_out=asum[:, KT + o:KT + o + 1]).then_inc(wf_used, 1)
                dve.wait_ge(wf_used, KT + o + 1)
            done(dve.tensor_reduce(tot_s, asum[:, 0:KT], AX.X, ALU.add))
            dve.tensor_reduce(tot_n, asum[:, KT:2 * KT], AX.X, ALU.add).then_inc(part_in, 1)

            for q in range(2):
                dve.wait_ge(tern_st[q], 16 * KT // 2)
            dve.sem_inc(oh_used, 2)

            def bc(ap, w):
                return ap.unsqueeze(2).to_broadcast([TP, NB, w])

            def io(w):
                return iota[0:TP, 0:w].unsqueeze(1).to_broadcast([TP, NB, w])

            with dve.Fori(0, 2) as i:
                for b20 in range(EC // NB // 2):
                    b = i * (EC // NB // 2) + b20
                    ohl, rhs, eq, ohlow, oh80 = batches[b20 % 2]
                    cols = lambda ap: ap[:, bass.ds(b * NB, NB)]
                    dve.wait_ge(oh_used, b + 1)
                    dve.tensor_tensor(eq, io(CH), bc(cols(pcf), CH), ALU.is_equal).then_inc(eq_ready, 1)
                    dve.tensor_tensor(ohl, io(P), bc(cols(plf), P), ALU.is_equal)
                    dve.tensor_tensor(ohlow, io(P), bc(cols(lowf), P), ALU.is_equal)
                    dve.tensor_tensor(oh80, io(NT * R), bc(cols(k80), NT * R), ALU.is_equal)
                    dve.wait_ge(eq_ready, b + 1)
                    dve.tensor_tensor(rhs[:, :, 0:CH], eq, bc(cols(srcf), CH), ALU.mult)
                    dve.tensor_tensor(rhs[:, :, CH:2 * CH], eq, bc(cols(bfld), CH), ALU.mult).then_inc(oh_ready, 1)

            dve.wait_ge(oh_used, EC // NB + 2)
            sv = big[:, 0:4 * CH].rearrange("p (a c) -> p a c", a=4)
            tabs = big[:, 2048:2048 + NT * R]
            tabs2 = big[:, 2560:2560 + CH]
            ti = sv[:, 2, :].bitcast(I32)
            tj = sv[:, 3, :].bitcast(I32)
            done(dve.memset(tabs, 0.0))
            done(dve.tensor_scalar(tabs[0:TP, :], cnt_b[0:TP, 0:NT * R], 1.0, None, ALU.max))
            dve.reciprocal(tabs[0:TP, :], tabs[0:TP, :]).then_inc(idx_ready, 1)
            done(dve.tensor_scalar(ti, perm_b[:, CH:2 * CH], -1.0, None, ALU.add))
            done(dve.tensor_scalar(tj, ti, P - 1, None, ALU.bitwise_and))
            low = tabs2
            done(dve.tensor_copy(low, tj))
            done(dve.tensor_scalar(tj, ti, 7, None, ALU.arith_shift_right))
            done(dve.tensor_copy(sv[:, 0, :], tj))
            done(dve.tensor_scalar(sv[:, 0, :], sv[:, 0, :], 0.0, None, ALU.max))
            done(dve.scalar_tensor_tensor(idx_all[:, 0, 0:CH], sv[:, 0, :], float(N), perm_b[:, 0:CH], ALU.mult, ALU.add))
            done(dve.scalar_tensor_tensor(sv[:, 1, :], low, float(NT * R), sv[:, 0, :], ALU.mult, ALU.add))
            done(dve.tensor_tensor(idx_all[:, 1, 0:CH], sv[:, 1, :], low_s[:, 0:CH], ALU.add))
            dve.tensor_copy(low_s[:, 0:CH], low).then_inc(idx_ready, 1)

            def edges(half):
                dve.wait_ge(agg_set, 16 * (half + 1))
                per = AHEAD
                with dve.Fori(0, PAIRS // per) as i:
                    for at in range(per):
                        for e in range(2):
                            c = i * (2 * per) + (2 * at + e)
                            s6 = 2 * (at % AHEAD) + e
                            dve.wait_ge(agg_mm, c + (half * CH + 1))
                            factor = w_slot[:, s6, :] if half == 0 else w_all[:, bass.ds(i * (2 * per) + (2 * at + e), 1)]
                            dve.tensor_scalar(onehot[:, e, 0:TP], iota[:, 0:TP], low_s[:, bass.ds(c, 1)], None, ALU.is_equal)
                            dve.wait_ge(msg_hi_done, c + (half * CH + 1))
                            dve.scalar_tensor_tensor(msg_lo[:, e, :], gath[:, s6, :], factor, f(msg_hi[:, e, :]),
                                                     ALU.mult, ALU.subtract).then_inc(msg_lo_done, 1)
                            if half == 0:
                                dve.tensor_copy(w_all[:, bass.ds(i * (2 * per) + (2 * at + e), 1)], w_slot[:, s6, :]
                                                ).then_inc(w_kept, 1)
                        for e in range(2):
                            c = i * (2 * per) + (2 * at + e)
                            v = dve.value_load(tile_i[0:1, bass.ds(c, 1)], min_val=0, max_val=NT - 1)
                            dve.wait_ge(agg_mm, c + (half * CH + 3))
                            dve.wait_ge(agg_added, c + (half * CH + 2))
                            acc = agg[0:TP, bass.ds(v, 1), :]
                            dve.tensor_tensor(acc, acc, ab[e][0:TP, :].unsqueeze(1), ALU.add).then_inc(agg_added, 1)

            edges(0)
            edges(1)

            done(dve.tensor_tensor(nmean[0:TP, :], mv[0:TP, :, 0], mv[0:TP, :, 1], ALU.mult))
            dve.tensor_scalar(nmean[0:TP, :], nmean[0:TP, :], -1.0, None, ALU.mult).then_inc(s_nm, 1)
            dve.wait_ge(s_bc, 48)
            for t in range(2):
                lo_half(dve, 2 * NT + 2 * t, t)
            mvt = sm[0:TP, 2:4]
            for t in range(NT):
                s = t % 2
                r, xx, z, xn = (b[s][0:TP, :] for b in (Rr, Xx, Zz, Xn))
                dve.wait_ge(base_ready, t + 1)
                for j in range(NH):
                    dve.wait_ge(gate_ready, 2 * t + j + 1)
                    dve.tensor_tensor(z[:, j * H:(j + 1) * H], yb[j][0:TP, :], z[:, j * H:(j + 1) * H], ALU.add
                                      ).then_inc(gate_taken, 1)
                dve.wait_ge(gate_taken, 2 * t + 2)
                done(dve.tensor_tensor(z, z, r, ALU.mult))
                dve.tensor_tensor(z, z, xx, ALU.add).then_inc(y2_ready, 1)
                if t + 2 < NT:
                    lo_half(dve, 2 * NT + 2 * (t + 2), t + 2)
                dve.wait_ge(y2_ready, t + 1)
                row_stats(z, mvt)
                done(dve.tensor_scalar(sm[0:TP, 1:2], mvt[:, 1:2], LN_EPS, LN_EPS, ALU.add, ALU.mult))
                dve.tensor_tensor(sm[0:TP, 0:1], sm[0:TP, 1:2], mvt[:, 1:2], ALU.add).then_inc(sd_ready, 1)
                if t >= 2:
                    dve.wait_ge(xn_out[s], 16 * (t // 2))
                done(dve.scalar_tensor_tensor(xn, z, mvt[:, 0:1], X0[0:TP, :], ALU.subtract, ALU.mult))
                dve.wait_ge(sd_done, t + 2)
                done(dve.reciprocal(sm[0:TP, 0:1], sm[0:TP, 0:1]))
                dve.tensor_copy(sm[0:TP, 1:2], sm[0:TP, 0:1]).then_inc(n_ready, 1)
                dve.scalar_tensor_tensor(xn, xn, sm[0:TP, 0:1], X1[0:TP, :], ALU.mult, ALU.add).then_inc(xn_ready, 1)
                dve.wait_ge(xn_ready, t + 1)
                dve.tensor_reduce(amax[0:TP, t:t + 1], xn, AX.X, ALU.max, apply_absolute_value=True).then_inc(xn_maxed, 1)
            dve.wait_ge(xn_maxed, NT)
            dve.tensor_reduce(gmx[0:TP, :], amax[0:TP, :], AX.X, ALU.max).then_inc(gm_in, 1)
            dve.wait_ge(part_out, 2)
            done(dve.tensor_scalar(tot_n, psums[:, 1:2], 1.0, None, ALU.max))
            done(dve.reciprocal(tot_n, tot_n))
            done(dve.tensor_tensor(alpha, psums[:, 0:1], tot_n, ALU.mult))
            dve.wait_ge(gm_out, 1)
            done(dve.tensor_scalar(gms[0:TP, :], gms[0:TP, :], 1e-8, 1.0 / 127.0, ALU.max, ALU.mult))
            done(dve.reciprocal(qinv[0:TP, :], gms[0:TP, :]))
            done(dve.tensor_tensor(outscale[0:TP, :], gms[0:TP, :], alpha[0:TP, :], ALU.mult))
            for t in range(NT + 2):
                if t < NT:
                    a = Xe[t % 3][0:TP, :]
                    dve.wait_ge(xe_in[t % 3], 16 * (t // 3 + 1))
                    done(dve.tensor_scalar(a, a, qinv[0:TP, :], 127.0, ALU.mult, ALU.min))
                    done(dve.tensor_scalar(a, a, -127.0, MAGIC, ALU.max, ALU.add))
                    if t >= 3:
                        dve.wait_ge(qt_ready, t - 2)
                    dve.tensor_scalar(Qb[t % 3][0:TP, :], a, -MAGIC, None, ALU.add).then_inc(q_ready, 1)
                if t >= 2:
                    m = t - 2
                    z = Ze[m % 3][0:TP, :]
                    dve.wait_ge(ze_in[m % 3], 16 * (m // 3 + 1))
                    for j in range(NH):
                        dve.wait_ge(f_ready, 2 * m + j + 1)
                        zj = z[:, j * H:(j + 1) * H]
                        dve.scalar_tensor_tensor(zj, fb[2 * (m % 2) + j][0:TP, :], outscale[0:TP, :], zj, ALU.mult, ALU.add
                                                 ).then_inc(f_done, 1)

        @block.gpsimd
        def _(pool):
            pool.iota(iota[:, :], pattern=[[1, CH]], base=0, channel_multiplier=0,
                      allow_small_or_imprecise_dtypes=True).then_inc(s_const, 1)
            pool.memset(idx_all[:, :, :], 0).then_inc(s_const, 1)
            for m in (ident, ident_b):
                pool.memset(m[:, :], 1.0).then_inc(s_const, 1)
            pool.wait_ge(s_const, 4)
            pool.affine_select(out=ident[:, :], in_=ident[:, :], compare_op=ALU.is_equal, fill=0.0, base=0,
                               pattern=[[-1, P]], channel_multiplier=1)
            pool.affine_select(out=ident_b[:, :], in_=ident_b[:, :], compare_op=ALU.is_equal, fill=0.0, base=0,
                               pattern=[[-1, P]], channel_multiplier=1).then_inc(s_const, 1)
            pool.sem_inc(agg_mm, 2)

            def w_split_lo(done_hi, s, k):
                pool.wait_ge(w_hi_done, done_hi)
                pool.tensor_tensor(w_lo[:, s, k, :], w_stage[:, k % STG, :], f(w_hi[:, s, k, :]), ALU.subtract
                                   ).then_inc(w_lo_done, 1)

            for k in range(KT):
                w_split_lo(k + 1, 0, k)

            def triangles():
                pool.wait_ge(tr_lo, 2 * NT)
                pool.memset(ones_b, 1.0)
                pool.memset(low_tri, 1.0).then_inc(s_const, 1)
                pool.wait_ge(s_const, 6)
                pool.affine_select(out=low_tri, in_=low_tri, compare_op=ALU.is_gt, fill=0.0, base=0,
                                   pattern=[[1, 128]], channel_multiplier=-1).then_inc(s_const, 1)

            def load_ffn(o):
                if o >= 2:
                    pool.wait_ge(wf_used, o - 1)
                if o >= KT:
                    pool.wait_ge(scratch_free, 1)
                pool.dma_start(T[o % 2], wffn[(o % KT) * P:(o % KT + 1) * P, :]).then_inc(s_wf[o % 2], 16)

            def part_sum(n):
                pool.wait_ge(part_in, n + 1)
                pool.partition_all_reduce(psums[:, 0:2], both, P, bass.bass_isa.ReduceOp.add).then_inc(part_out, 1)

            def gather_pair(p, r3, half):
                pool.tensor_copy(idx_slot[:, r3, 0:2 - half, :], idx_all[:, 0:2 - half, bass.ds(p * 2, 2)]).then_inc(icopy, 1)
                pool.wait_ge(icopy, p + (half * CHX // 2 + 1))
                pool.sem_inc(icopy_seen, 1)
                for e in range(2):
                    s6 = 2 * r3 + e
                    if half == 0:
                        pool.indirect_dma_start(out=w_slot[:, s6, :], out_offset=None, in_=inv_dram,
                                                in_offset=bass.IndirectOffsetOnAxis(ap=idx_slot[:, r3, 1, e:e + 1], axis=0)
                                                ).then_inc(gw_landed[s6], 16)
                    pool.indirect_dma_start(out=gath[:, s6, :], out_offset=None, in_=y_dram[half],
                                            in_offset=bass.IndirectOffsetOnAxis(ap=idx_slot[:, r3, 0, e:e + 1], axis=0)
                                            ).then_inc(g_landed[s6], 16)

            def set_agg(half):
                pool.dma_start(agg[0:TP, :, :], bias[half * H:(half + 1) * H].unsqueeze(0).unsqueeze(0).to_broadcast([TP, NT, H])
                               ).then_inc(agg_set, 16)

            for n, (first, iters, pairs, half) in enumerate(LOOPS):
                if n == 3:
                    pool.wait_ge(idx_ready, 1)
                    pool.dma_start(inv_dram.rearrange("(p c) o -> p (c o)", p=P), big[:, 2048:2048 + NT * R]).then_inc(s_inv, 16)
                    pool.wait_ge(s_inv, 16)
                    pool.wait_ge(idx_ready, 2)
                    set_agg(0)
                if n in (3, 4):
                    for q in range(2):
                        pool.wait_ge(y_stored[q], 16 * (half + 1) * R * NT // 2)
                    for p in range(AHEAD):
                        if half == 1:
                            pool.wait_ge(msg_lo_done, CH)
                            pool.wait_ge(w_kept, CH)
                            for e in range(2):
                                pool.wait_ge(g_landed[2 * p + e], 16 * CHX // GS)
                                pool.wait_ge(gw_landed[2 * p + e], 16 * CHX // GS)
                        gather_pair(p, p, half)
                if n == 4:
                    pool.wait_ge(agg_added, CH + 2)
                    pool.dma_start(agg_dram.rearrange("(t p) c -> p t c", p=TP), agg[0:TP, :, :]).then_inc(agg_out, 16)
                    pool.wait_ge(agg_out, 16)
                    set_agg(1)
                if n == 5:
                    for q in range(2):
                        pool.wait_ge(y_stored[q], 16 * 18 * NT // 2)
                    pool.dma_start(rz_dram[0:N, :], agg_dram, accum_op=ALU.add, max_dma_last_dim=4 * H).then_inc(u_summed[0][0], 16)
                with loop(pool, iters) as i:
                    for s in range(2):
                        u = i * 2 + (first + s)
                        for m in range(NT):
                            for p in with_pairs(n, s, m):
                                q = before(n) + p
                                if half == 1 and q + AHEAD >= PAIRS:
                                    continue
                                pool.wait_ge(msg_lo_done, i * (2 * sum(pairs)) + (2 * (q + 1) + half * CH))
                                if half == 0:
                                    pool.wait_ge(w_kept, i * (2 * sum(pairs)) + 2 * (q + 1))
                                gather_pair(i * sum(pairs) + (q + AHEAD), q % AHEAD, half)
                            if 1 <= m <= KT:
                                w_split_lo(u * KT + (KT + m), 1 - s, m - 1)
                            if n == 0 and s == 0 and m == 5:
                                triangles()
                            if n == 0 and s == 0 and 6 <= m:
                                load_ffn(2 * m - 12)
                                load_ffn(2 * m - 11)
                            if n == 0 and (s, m) == (1, 2):
                                part_sum(0)
                            if n == 1 and s == 0 and m < KT:
                                load_ffn(KT + m)
                            if n == 1 and (s, m) == (1, NT - 1):
                                part_sum(1)
            pool.wait_ge(agg_added, 2 * CH + 2)
            for t in range(NT):
                pool.dma_start(rz_dram[N + t * TP:N + (t + 1) * TP, :], agg[0:TP, t, :], accum_op=ALU.add).then_inc(u_summed[1][t], 16)
            for k in range(KT):
                w_split_lo(21 * KT + k + 1, 1, k)
            for q in range(2):
                pool.wait_ge(y_stored[q], 16 * 20 * NT // 2)
            for ap, dest in ((bgate, EV), (gamma, X0), (beta, X1)):
                pool.dma_start(dest[0:TP, :], ap.unsqueeze(0).to_broadcast([TP, D])).then_inc(s_bc, 16)
            pool.wait_ge(s_bc, 48)
            for t in range(NT):
                s = t % 2
                a, xx, r, z = (b[s][0:TP, :] for b in (A, Xx, Rr, Zz))
                pool.wait_ge(xl2_ready, t + 1)
                pool.tensor_tensor(r, r, a, ALU.subtract)
                pool.tensor_tensor(xx, xx, a, ALU.add)
                pool.wait_ge(z_in[s], 16 * (t // 2 + 1))
                pool.tensor_tensor(z, z, EV[0:TP, :], ALU.add).then_inc(base_ready, 1)
            pool.wait_ge(gm_in, 1)
            pool.partition_all_reduce(gms[0:TP, :], gmx[0:TP, :], TP, bass.bass_isa.ReduceOp.max).then_inc(gm_out, 1)


def kernel(**inputs):
    import numpy as np
    from concourse import bacc
    from concourse.bass_utils import run_bass_kernel_spmd

    a = {k: np.asarray(v) for k, v in inputs.items()}
    rel, root, wg = a["L0_gnn_weight"], a["L0_gnn_root"], a["L0_gnn_w_gate"]
    mats = [(rel[r], j) for j in range(NH) for r in range(R)]
    mats += [(m, j) for m in (root, wg[D:], wg[:D]) for j in range(NH)]
    wall = np.concatenate([m[:, j * H:(j + 1) * H] for m, j in mats], axis=0)
    arrays = {
        "x": a["x"], "src": a["src"], "dst": a["dst"], "edge_type": a["edge_type_8"], "weights": wall,
        "bias": a["L0_gnn_bias"], "b_gate": a["L0_gnn_b_gate"], "ffn_weight": a["L0_ffn_weight"],
        "ffn_gamma": a["L0_ffn_gamma"], "ffn_beta": a["L0_ffn_beta"],
    }
    arrays = {k: np.ascontiguousarray(v) for k, v in arrays.items()}
    nc = bacc.Bacc("TRN2", target_bir_lowering=False, num_devices=1)
    args = [nc.dram_tensor(f"in_{k}", v.shape, mybir.dt.from_np(v.dtype), kind="ExternalInput").ap()
            for k, v in arrays.items()]
    args.append(nc.dram_tensor("out_y", (N, D), F32, kind="ExternalOutput").ap())
    build(nc, *args)
    r = run_bass_kernel_spmd(nc, [{f"in_{k}": v for k, v in arrays.items()}], core_ids=[0])
    return r.results[0]["out_y"]
```

```python
import contextlib
from contextlib import ExitStack

import concourse.bass as bass
from concourse import mybir

F32, F32R = mybir.dt.float32, mybir.dt.float32r
F16, BF16, I32 = mybir.dt.float16, mybir.dt.bfloat16, mybir.dt.int32
ALU = mybir.AluOpType
ACT = mybir.ActivationFunctionType
AX = mybir.AxisListType

P = 128
N, D, R, E = 1250, 1024, 8, 20000
TP = 125
NT = N // TP
KT = D // P
H = 512
NH = D // H
EC = E // TP
PAIRS = (E + NT * (2 * P - 1)) // (2 * P)
CH = 2 * PAIRS
AHEAD = 4
GS = 2 * AHEAD
CHX = CH + GS
STG = 4
NB = 5
LN_EPS = 1e-5
MAGIC = 1.5 * 2.0 ** 23
assert PAIRS % AHEAD == 0 and EC % NB == 0


def build(nc, x, src, dst, etype, wall, bias, bgate, wffn, gamma, beta, out):
    ctx = ExitStack()
    with ctx:
        def sb(name, shape, dt):
            return ctx.enter_context(nc.sbuf_tensor(name, shape, dt))

        def sem(name):
            return ctx.enter_context(nc.semaphore(name))

        y_dram = [nc.dram_tensor(f"y_dram{j}", [R * N, H], F32, kind="Internal").ap() for j in range(NH)]
        rz_dram = nc.dram_tensor("rz_dram", [2 * NH * N, H], F32, kind="Internal").ap()
        agg_dram = nc.dram_tensor("agg_dram", [N, H], F32, kind="Internal").ap()
        inv_dram = nc.dram_tensor("inv_dram", [P * NT * R, 1], F32, kind="Internal").ap()
        tern_dram = nc.dram_tensor("tern_dram", [KT * P, D], BF16, kind="Internal").ap()
        y2_dram = nc.dram_tensor("y2_dram", [N, D], F32, kind="Internal").ap()
        xn_dram = nc.dram_tensor("xn_dram", [N, D], F32, kind="Internal").ap()

        xt_hi = sb("xt_hi", [P, KT, N], F32R)
        xt_lo = sb("xt_lo", [P, KT, N], F32R)
        w_hi = sb("w_hi", [P, 2, KT, H], F32R)
        w_lo = sb("w_lo", [P, 2, KT, H], F32R)
        w_stage = sb("w_stage", [P, STG, H], F32)
        agg = sb("agg", [P, NT, H], F32)
        gath = sb("gath", [P, 6, H], F32)
        msg_hi = sb("msg_hi", [P, 2, H], F32R)
        msg_lo = sb("msg_lo", [P, 2, H], F32R)
        onehot = sb("onehot", [P, 2, TP + 1], F32R)
        evict = sb("evict", [P, 2, H], F32)
        extra = sb("extra", [P, 2 * D], F32)
        idx_all = sb("idx_all", [P, 2, CHX], I32)
        low_s = sb("low_s", [P, CHX], F32)
        tile_i = sb("tile_i", [1, CHX // 2], mybir.dt.int16)
        iota = sb("iota", [P, CH], F32)
        ident = sb("ident", [P, P], F32)
        ident_b = sb("ident_b", [P, P], BF16)
        idx_slot = sb("idx_slot", [P, AHEAD, 2, 2], I32)
        w_slot = sb("w_slot", [P, GS, 1], F32)
        mv = sb("mv", [P, NT, 2], F32)
        stats = sb("stats", [P, 2, 6], F32)
        sm = sb("sm", [P, 64], F32)
        amax = sb("amax", [P, NT], F32)

        def bank(name):
            return ctx.enter_context(nc.psum_tensor(name, [P, H], F32))
        yb = [bank("yb0"), bank("yb1")]
        ab = [bank("ab0"), bank("ab1")]
        tb = [bank("tb0"), bank("tb1")]
        perm_b, cnt_b = bank("perm_b"), bank("cnt_b")
        fb = yb + ab
        gb = [yb, ab]
        mb = ab + [perm_b, cnt_b]
        MB = len(mb)

        big = agg[:, :, :].rearrange("p t c -> p (t c)")
        gbig = gath[:, :, :].rearrange("p s c -> p (s c)")
        T = [big[:, i * D:(i + 1) * D] for i in range(5)]
        G = [gbig[:, i * D:(i + 1) * D] for i in range(3)]
        EV = evict[:, :, :].rearrange("p s c -> p (s c)")
        X0, X1 = extra[:, 0:D], extra[:, D:2 * D]
        gslot = [gath[:, i, :] for i in range(6)] + [extra[:, i * H:(i + 1) * H] for i in range(2)]
        U_left = [extra[:, i * H:(i + 1) * H] for i in (2, 3, 0, 1)]

        s_const = sem("s_const")
        s_x = [sem(f"s_x{t}") for t in range(NT)]
        s_dve = sem("s_dve")
        xl_ready = sem("xl_ready")
        tr_ready = sem("tr_ready")
        tr_hi = sem("tr_hi")
        tr_lo = sem("tr_lo")
        sd_ready = sem("sd_ready")
        sd_done = sem("sd_done")
        s_edges = sem("s_edges")
        oh_tile = sem("oh_tile")
        rank_ready = sem("rank_ready")
        rank_used = sem("rank_used")
        s_wf = [sem("s_wf0"), sem("s_wf1")]
        wf_used = sem("wf_used")
        tern_ready = sem("tern_ready")
        tern_t = sem("tern_t")
        tern_c = sem("tern_c")
        tern_st = [sem("tern_st0"), sem("tern_st1")]
        part_in = sem("part_in")
        part_out = sem("part_out")
        w_landed = [sem(f"w_landed{i}") for i in range(STG)]
        w_first = [sem(f"w_first{k}") for k in range(KT)]
        w_hi_done = sem("w_hi_done")
        w_lo_done = sem("w_lo_done")
        last_lo = sem("last_lo")
        y_ready = sem("y_ready")
        y_free = sem("y_free")
        y_stored = [sem("y_stored0"), sem("y_stored1")]
        oh_ready = sem("oh_ready")
        oh_used = sem("oh_used")
        eq_ready = sem("eq_ready")
        idx_ready = sem("idx_ready")
        s_inv = sem("s_inv")
        scratch_free = sem("scratch_free")
        agg_set = sem("agg_set")
        agg_out = sem("agg_out")
        icopy = sem("icopy")
        icopy_seen = sem("icopy_seen")
        g_landed = [sem(f"g_landed{i}") for i in range(GS)]
        gw_landed = [sem(f"gw_landed{i}") for i in range(GS)]
        msg_hi_done = sem("msg_hi_done")
        msg_lo_done = sem("msg_lo_done")
        agg_mm = sem("agg_mm")
        agg_added = sem("agg_added")
        root_added = sem("root_added")
        ul_in = sem("ul_in")
        ul2_in = sem("ul2_in")
        s_bg = sem("s_bg")
        ur_out = sem("ur_out")
        w_kept = sem("w_kept")
        u_summed = sem("u_summed")
        a_in = [sem("a_in0"), sem("a_in1")]
        x_in = [sem("x_in0"), sem("x_in1")]
        z_in = [sem("z_in0"), sem("z_in1")]
        y2_out = [sem("y2_out0"), sem("y2_out1")]
        xn_out = [sem("xn_out0"), sem("xn_out1")]
        s_nm = sem("s_nm")
        th_done = sem("th_done")
        xl2_ready = sem("xl2_ready")
        lnx_used = sem("lnx_used")
        base_step = sem("base_step")
        base_ready = sem("base_ready")
        s_bc = sem("s_bc")
        gate_ready = [sem("gate_ready0"), sem("gate_ready1")]
        gate_taken = sem("gate_taken")
        y2_ready = sem("y2_ready")
        n_ready = sem("n_ready")
        xn_ready = sem("xn_ready")
        xn_maxed = sem("xn_maxed")
        gm_in = sem("gm_in")
        gm_out = sem("gm_out")
        s_tern = sem("s_tern")
        xe_in = [sem(f"xe_in{q}") for q in range(NT)]
        ze_in = [sem(f"ze_in{q}") for q in range(NT)]
        q_ready = sem("q_ready")
        qt_ready = sem("qt_ready")
        qt_done = sem("qt_done")
        f_ready = sem("f_ready")
        f_done = sem("f_done")
        o_out = [sem(f"o_out{q}") for q in range(4)]

        ex = [extra[0:TP, i * EC:(i + 1) * EC] for i in range(12)]
        srcf, dstf, typf, tile_a, tile_b, lowf, bfld, k80, pcf, plf = ex[2:12]
        ei = [ex[i].bitcast(I32) for i in (0, 1)]
        C16 = NT * EC
        cumT, cumI = big[:, 0:C16], big[:, C16:2 * C16]
        rankV = big[0:TP, 2 * C16:3 * C16]
        g16 = gbig[0:TP, :].bitcast(BF16)
        oh_t, low_tri, ones_b = g16[:, 0:C16], g16[:, C16:C16 + 128], g16[:, C16 + 128:C16 + 256]
        G2b = T[2]
        tern_out = [T[3].bitcast(BF16)[:, q * D:(q + 1) * D] for q in range(2)]
        big16 = big[0:TP, :].bitcast(F16)
        w_all = idx_all[:, 1, :].bitcast(F32)
        OHW = NB * (P + 2 * CH + CH + TP + 3 + NT * R)

        def batch_slot(s):
            at, res = s * OHW, []
            for w in (P, 2 * CH, CH, TP + 3, NT * R):
                res.append(big16[:, at:at + NB * w].rearrange("p (c w) -> p c w", c=NB))
                at += NB * w
            return res
        batches = [batch_slot(0), batch_slot(1)]

        tern_v = [gbig.bitcast(BF16)[:, i * D:(i + 1) * D] for i in range(6)] + \
                 [T[4].bitcast(BF16)[:, i * D:(i + 1) * D] for i in range(2)]
        tern_w = [q.bitcast(BF16).rearrange("p (o k c) -> p o k c", o=KT // 2, k=KT) for q in (big[:, 3 * D:5 * D], gbig[:, 0:2 * D])]

        WS = w_stage[:, :, :].rearrange("p s c -> p (s c)")
        A = [G[0], G[1]]
        Xx = [G[2], T[0]]
        Rr = [T[3], T[4]]
        Zz = [T[1], T[2]]
        Xn = [WS[:, 0:D], WS[:, D:2 * D]]
        xt_f = [xt[:, :, :].rearrange("p k n -> p (k n)").bitcast(F32) for xt in (xt_lo, xt_hi)]
        Xe, Ze = ([*last] + [b[:, v * D:(v + 1) * D] for v in range(NT - 2)] for last, b in zip((Xn, Zz), xt_f))
        Oe = [Zz[0], Zz[1], Xn[0], Xn[1]]
        Qf = [Xx[0], Xx[1]]
        E_ORDER = [NT - 2, NT - 1] + list(range(NT - 2))
        exb, evb = extra[:, :].bitcast(BF16), EV.bitcast(BF16)
        Qb = [exb[:, 0:D], exb[:, D:2 * D], exb[:, 2 * D:3 * D]]
        qT = [q[:, 0:KT * TP].rearrange("p (k n) -> p k n", k=KT) for q in (exb[:, 3 * D:4 * D], evb[:, 0:D])]
        XA = T + G + [X0, X1]
        TRANSPOSE_AT = {(0, 1): 1, (1, 5): 2, (2, 3): 3, (3, 3): 4, (4, 5): 5, (5, 1): 6, (5, 5): 7, (6, 1): 8, (6, 5): 9}
        LN_GROUPS = ((0, 2), (2, 5), (5, NT))
        first_stage = [w_stage[:, 2, :], w_stage[:, 3, :], evict[:, 0, :], evict[:, 1, :]] + [w_stage[:, k, :] for k in range(STG)]

        cntt, capt, base, delta_t, cap_i, tmp10 = (sm[:, 10 * i:10 * i + 10] for i in range(6))
        one_rstd = capt
        smc = lambda i: sm[:, 60 + i:61 + i]
        nmean = amax
        asum = sb("asum", [P, 2 * KT + 7], F32)
        thr, nthr, alpha = asum[:, 2 * KT:2 * KT + 1], asum[:, 2 * KT + 1:2 * KT + 2], asum[:, 2 * KT + 2:2 * KT + 3]
        tot_s, tot_n = asum[:, 2 * KT + 3:2 * KT + 4], asum[:, 2 * KT + 4:2 * KT + 5]
        both = asum[:, 2 * KT + 3:2 * KT + 5]
        psums = asum[:, 2 * KT + 5:2 * KT + 7]
        gmx, qinv = smc(0), smc(1)
        outscale, gms = smc(2), smc(3)

        rows = lambda ap, t: ap[t * TP:(t + 1) * TP, :]
        rz_v = rz_dram.rearrange("(u n) c -> n u c", u=2 * NH)
        f = lambda ap: ap.bitcast(F32)

        pairs_b1 = [0] * 2 + [1 + ((k + 1) * 9 // 35 - k * 9 // 35) for k in range(4 * NT - 5)] + [0] * 3
        pairs_c1 = [0] * 2 + [3, 2] * (NT - 1)
        pairs_c2 = [3, 2] * (NT - 2) + [3] + [0] * 3
        assert 2 * sum(pairs_b1) == PAIRS and sum(pairs_c1) + sum(pairs_c2) == PAIRS
        LOOPS = (
            (0, 1, 2, None, None),
            (2, 1, 2, None, None),
            (4, 2, 2, None, None),
            (8, 2, 4, pairs_b1, 0),
            (16, 1, 2, pairs_c1, 1), (18, 1, 2, pairs_c2, 1))
        ROOT_R = 17

        def stored(u):
            return (u - 1 if isinstance(u, int) and u > ROOT_R else u) * NT

        def loop(eng, iters):
            return eng.Fori(0, iters) if iters > 1 else contextlib.nullcontext(0)

        def sorts(n, s, m):
            return n == 2 and s * NT + m < EC // NB // 2

        block = ctx.enter_context(nc.Block())

        def with_pairs(n, s, m):
            pairs = LOOPS[n][3]
            if pairs is None:
                return []
            at = sum(pairs[:s * NT + m])
            return range(at, at + pairs[s * NT + m])

        def with_chunks(n, s, m):
            pairs = with_pairs(n, s, m)
            if not pairs:
                return []
            first, last = 2 * pairs[0], 2 * (pairs[-1] + 1)
            if LOOPS[n][4] == 1:
                if len(pairs) == 2:
                    first -= 1
                elif last < 2 * sum(LOOPS[n][3]):
                    last -= 1
            return range(first, last)

        def places(count):
            return PLACES.get(count, [KT - 1 - (count - 1 - q) * 6 // count for q in range(count)])
        PLACES = {5: (1, 3, 4, 6, 7)}

        def before(n):
            return sum(lp[1] * sum(lp[3]) for lp in LOOPS[:n] if lp[3] and lp[4] == LOOPS[n][4])

        def lo_half(dve, n0, t):
            for h in range(2):
                dve.wait_ge(tr_hi, n0 + h + 1)
                dst3 = (xt_lo[:, 4 * h:4 * h + 4, t * TP:(t + 1) * TP])
                hi3 = f(xt_hi[:, 4 * h:4 * h + 4, t * TP:(t + 1) * TP])
                dve.tensor_tensor(dst3, tb[h][:, 0:4 * TP].rearrange("p (k n) -> p k n", k=4), hi3,
                                  ALU.subtract).then_inc(tr_lo, 1)

        @block.sync
        def _(sp):
            def load_w(g, k):
                sp.dma_start(w_stage[:, k % STG, :], wall[g * P:(g + 1) * P, :]).then_inc(w_landed[k % STG], 16)

            def load_x(t):
                sp.dma_start(XA[t][0:TP, :], rows(x, t)).then_inc(s_x[t], 16)

            def load_first(k):
                if k >= 6:
                    sp.wait_ge(w_lo_done, k - 5)
                sp.dma_start(first_stage[k], wall[k * P:(k + 1) * P, :]).then_inc(w_first[k], 16)

            for t in range(2):
                load_x(t)
                load_first(t)
            for k in range(2, 6):
                load_first(k)
            load_x(2)
            load_first(6)
            load_x(3)
            load_first(7)
            for t in range(4, NT):
                load_x(t)

            for n, (first, iters, units, _, half) in enumerate(LOOPS):
                table, t0 = ((y_dram[0], 0), (y_dram[1], 8), (rz_dram, 16))[0 if first < 8 else 1 if first < 16 else 2]
                with loop(sp, iters) as i:
                    for s in range(units):
                        u = i * units + (first + s)
                        for m in range(NT):
                            if m < KT:
                                sp.wait_ge(w_lo_done, u * KT + (KT + m - STG + 1))
                                sp.dma_start(w_stage[:, m % STG, :], wall[bass.ds(u * (KT * P) + (KT + m) * P, P), :]
                                             ).then_inc(w_landed[m % STG], 16)
                            if n == 0 and s == 0 and m == 7:
                                sp.wait_ge(tr_lo, 2 * NT)
                                for a, t in ((src, ei[0]), (dst, ei[1]), (etype, ex[11].bitcast(I32))):
                                    sp.dma_start(t, a.rearrange("(p c) -> p c", p=TP)).then_inc(s_edges, 16)
                            if (n, s) != (4, 1):
                                sp.wait_ge(y_free, stored(u) + (m + 3))
                                sp.dma_start(table[bass.ds(i * (units * N) + ((first - t0 + s) * N + m * TP), TP), :],
                                             evict[0:TP, m % 2, :]).then_inc(y_stored[m % 2], 16)
                            if (n, s, m) == (5, 0, 4):
                                sp.wait_ge(u_summed, 16)
                                for t in range(2):
                                    sp.dma_start(U_left[t][0:TP, :], rz_dram[t * TP:(t + 1) * TP, :]).then_inc(ul_in, 16)
                            if (n, s) == (5, 1) and m >= 6:
                                sp.wait_ge(w_lo_done, 21 * KT + m - 6 - STG + 1)
                                load_w(21 * KT + m - 6, m - 6)
                            if (n, s, m) == (5, 1, 8):
                                sp.wait_ge(agg_added, 2 * PAIRS + MB)
                                for t in (2, 3):
                                    sp.dma_start(U_left[t][0:TP, :], rz_dram[t * TP:(t + 1) * TP, :]).then_inc(ul2_in, 16)
                                sp.dma_start(rz_dram[N:2 * N, :].rearrange("(t p) c -> p t c", p=TP), agg[0:TP, :, :]
                                             ).then_inc(ur_out, 16)
                            if n == 1 and s == 1 and m < KT:
                                sp.wait_ge(tern_c, m + 1)
                                sp.dma_start(tern_dram[m * P:(m + 1) * P, :], tern_out[m % 2]
                                             ).then_inc(tern_st[m % 2], 16)
            def load_u(t):
                sp.dma_start(A[t % 2][0:TP, :].rearrange("p (u c) -> p u c", u=2), rz_v[t * TP:(t + 1) * TP, 0:2, :]
                             ).then_inc(a_in[t % 2], 16)

            def load_xd(t):
                sp.dma_start(Xx[t % 2][0:TP, :], rows(x, t)).then_inc(x_in[t % 2], 16)

            def load_z(t):
                sp.dma_start(Zz[t % 2][0:TP, :].rearrange("p (u c) -> p u c", u=2), rz_v[t * TP:(t + 1) * TP, 2:4, :]
                             ).then_inc(z_in[t % 2], 16)
            load_xd(0)
            sp.wait_ge(ur_out, 16)
            sp.wait_ge(tr_ready, 2 * NT + 8)
            load_z(0)
            sp.dma_start(X0[0:TP, :], gamma.unsqueeze(0).to_broadcast([TP, D])).then_inc(s_bc, 16)
            sp.wait_ge(th_done, 2)
            load_xd(1)
            load_z(1)
            sp.dma_start(X1[0:TP, :], beta.unsqueeze(0).to_broadcast([TP, D])).then_inc(s_bc, 16)
            for k in range(STG, KT):
                sp.wait_ge(last_lo, k - STG + 1)
                load_w(21 * KT + k, k)
            for t in range(2, NT + 2):
                s = t % 2
                if t < NT:
                    sp.wait_ge(lnx_used, t - 1)
                    load_u(t)
                    sp.wait_ge(base_ready, 2 * (t - 1))
                    load_xd(t)
                if 2 <= t < NT:
                    sp.wait_ge(y2_ready, 2 * (t - 1))
                    sp.dma_start(rows(y2_dram, t - 2), Zz[s][0:TP, :]).then_inc(y2_out[s], 16)
                    sp.wait_ge(y2_out[s], 16 * (t // 2))
                    sp.wait_ge(n_ready, t - 1)
                if t < NT:
                    load_z(t)
                if 2 <= t < NT:
                    sp.wait_ge(xn_ready, t - 1)
                    sp.dma_start(rows(xn_dram, t - 2), Xn[s][0:TP, :]).then_inc(xn_out[s], 16)

            ternary = tern_dram.rearrange("(o p) c -> p o c", p=P)
            sp.wait_ge(base_ready, 2 * NT)
            sp.wait_ge(xl2_ready, NT)
            sp.dma_start(tern_w[1].rearrange("p o k c -> p o (k c)"), ternary[:, 4:8, :]).then_inc(s_tern, 16)
            sp.wait_ge(y2_ready, 2 * NT)
            sp.dma_start(tern_w[0].rearrange("p o k c -> p o (k c)"), ternary[:, 0:4, :]).then_inc(s_tern, 16)
            for q in range(2):
                sp.wait_ge(gate_ready[q], NT)
                sp.wait_ge(y2_out[q], 16 * (NT // 2 - 1))
            for v in range(2, NT):
                sp.dma_start(Ze[v][0:TP, :], rows(y2_dram, E_ORDER[v])).then_inc(ze_in[v], 16)
            for v in range(NT):
                sp.wait_ge(f_done, 2 * (v + 1))
                sp.dma_start(rows(out, E_ORDER[v]), Oe[v % 4][0:TP, :]).then_inc(o_out[v % 4], 16)
            for q in range(4):
                sp.wait_ge(o_out[q], 16 * ((NT + 3 - q) // 4))

        @block.tensor
        def _(pe):
            def transpose_tile(src_tile, n0):
                for h in range(2):
                    if n0 + h >= 2:
                        pe.wait_ge(tr_lo, n0 + h - 1)
                    for q in range(4):
                        ins = pe.transpose(tb[h][:, q * TP:(q + 1) * TP],
                                           src_tile[0:TP, (4 * h + q) * P:(4 * h + q + 1) * P], ident[0:TP, 0:TP])
                    ins.then_inc(tr_ready, 1)

            def transpose_u(t):
                for h, part in enumerate((U_left[t][0:TP, :], agg[0:TP, t, :])):
                    pe.wait_ge(tr_lo, 2 * NT + 2 * t + h - 1)
                    for q in range(4):
                        ins = pe.transpose(tb[h][:, q * TP:(q + 1) * TP], part[:, q * P:(q + 1) * P], ident[0:TP, 0:TP])
                    ins.then_inc(tr_ready, 1)

            def ranks():
                w2 = 2 * EC
                pe.wait_ge(s_const, 7)
                pe.wait_ge(oh_tile, 1)
                for q in range(NT // 2):
                    for n, tri, m in ((2 * q, ones_b, P), (2 * q + 1, low_tri, TP)):
                        if n >= 2:
                            pe.wait_ge(rank_used, n - 1)
                        pe.matmul(ab[n % 2][0:m, 0:w2], tri[:, 0:m], oh_t[:, q * w2:(q + 1) * w2], start=True, stop=True
                                  ).then_inc(rank_ready, 1)

            def chunk(c, e, pair, b):
                pe.wait_ge(msg_lo_done, c + 1)
                if e == 0:
                    pe.wait_ge(agg_added, pair + 1)
                pe.matmul(mb[b][0:TP, :], onehot[:, e, 0:TP], msg_hi[:, e, :], start=e == 0, stop=False)
                pe.matmul(mb[b][0:TP, :], onehot[:, e, 0:TP], msg_lo[:, e, :], start=False, stop=e == 1
                          ).then_inc(agg_mm, 1)

            def sort_batch(b, s):
                ohl, rhs, _, ohlow, oh80 = batches[s]
                pe.wait_ge(oh_ready, b + 1)
                for c in range(NB):
                    end = c == NB - 1
                    pe.matmul(perm_b[:, 0:2 * CH], ohl[:, c, :], rhs[:, c, :], start=False, stop=end, skip_group_check=True)
                    ins = pe.matmul(cnt_b[0:TP, 0:NT * R], ohlow[:, c, 0:TP], oh80[:, c, :], start=False, stop=end,
                                    skip_group_check=True)
                ins.then_inc(oh_used, 1)

            def products(bank_j, s, k, m):
                xh, xl = xt_hi[:, k, m * TP:(m + 1) * TP], xt_lo[:, k, m * TP:(m + 1) * TP]
                o = bank_j[0:TP, :]
                pe.matmul(o, xh, w_hi[:, s, k, :], start=k == 0, stop=False)
                pe.matmul(o, xh, w_lo[:, s, k, :], start=False, stop=False)
                return pe.matmul(o, xl, w_hi[:, s, k, :], start=False, stop=k == KT - 1)

            pe.wait_ge(s_const, 5)
            for n, (first, iters, units, pairs, half) in enumerate(LOOPS):
                with loop(pe, iters) as i:
                    for s in range(units):
                        for m in range(NT):
                            u = i * units + (first + s)
                            if n == 0 and s == 0:
                                if m == 0:
                                    pe.wait_ge(xl_ready, 1)
                                    transpose_tile(XA[0], 0)
                                pe.wait_ge(tr_lo, 2 * (m + 1))
                            todo = [(i * (2 * sum(pairs)) + (2 * before(n) + c + half * CH), c % 2,
                                     i * sum(pairs) + (before(n) + c // 2 + half * PAIRS), (before(n) + c // 2) % MB)
                                    for c in with_chunks(n, s, m)]
                            if (n, s) == (4, 1) and m >= 2:
                                pe.wait_ge(root_added, m - 1)
                            elif (n, s) == (5, 0) and m < 2:
                                pe.wait_ge(root_added, NT - 1 + m)
                            else:
                                pe.wait_ge(y_free, stored(u) + (m + 1))
                            gaps = {}
                            for q in range(len(todo)):
                                gaps.setdefault(places(len(todo))[q], []).append(todo[q])
                            for k in range(KT):
                                if m == 0:
                                    pe.wait_ge(w_lo_done, u * KT + (k + 1))
                                ins = products(yb[m % 2], s % 2, k, m)
                                if k == KT - 1:
                                    ins.then_inc(y_ready, 1)
                                for c in gaps.get(k, []):
                                    chunk(*c)
                                if n == 0 and s == 0 and (m, k) in TRANSPOSE_AT:
                                    t = TRANSPOSE_AT[m, k]
                                    pe.wait_ge(xl_ready, t + 1)
                                    transpose_tile(XA[t], 2 * t)
                            if n == 0 and (s, m) == (1, 3):
                                ranks()
                            if n == 1 and s == 1 and m < KT:
                                pe.wait_ge(tern_ready, m + 1)
                                if m >= 2:
                                    pe.wait_ge(tern_c, m - 1)
                                tbb = tb[m % 2][:, :].bitcast(BF16)
                                for k in range(KT):
                                    ins = pe.transpose(tbb[:, k * P:(k + 1) * P], tern_v[m][:, k * P:(k + 1) * P], ident_b[:, :])
                                ins.then_inc(tern_t, 1)
                            if n == 1 and (s, m) == (1, NT - 1):
                                z = idx_all[:, :, :].rearrange("p a c -> p (a c)").bitcast(F16)
                                pe.matmul(perm_b[:, 0:2 * CH], z[:, 0:P], z[:, 0:2 * CH], start=True, stop=True)
                                pe.matmul(cnt_b[0:TP, 0:NT * R], z[:, 0:TP], z[:, 0:NT * R], start=True, stop=True)
                            if sorts(n, s, m):
                                sort_batch(i * (EC // NB // 2) + (s * NT + m), m % 2)
                            if (n, s) == (5, 1) and m in (7, 8):
                                pe.wait_ge(ul_in, 32)
                                pe.wait_ge(agg_added, 2 * PAIRS + MB)
                                transpose_u(m - 7)

            def gate(t, j):
                pe.wait_ge(tr_lo, 2 * NT + 2 * (t + 1))
                if t >= 2:
                    pe.wait_ge(gate_taken, 2 * (t - 2) + j + 1)
                for k in range(KT):
                    if t == 0 and j == 0:
                        pe.wait_ge(w_lo_done, 20 * KT + k + 1)
                    elif t == 0:
                        pe.wait_ge(last_lo, k + 1)
                    ins = products(gb[t % 2][j], j, k, t)
                ins.then_inc(gate_ready[j], 1)

            def transpose_a(t):
                pe.wait_ge(a_in[t % 2], 16 * (t // 2))
                transpose_tile(A[t % 2], 2 * NT + 2 * t)
            pe.wait_ge(y_free, stored(20) + 2)
            pe.wait_ge(ul2_in, 32)
            for t in (2, 3):
                transpose_u(t)
            for t, j in ((0, 0), (1, 0), (0, 1), (1, 1)):
                gate(t, j)
            for t in range(2, NT):
                gate(t, 0)
                if 2 < t < NT - 1:
                    transpose_a(t + 1)
                gate(t, 1)

            def transpose_q(t):
                pe.wait_ge(q_ready, t + 1)
                if t >= 2:
                    pe.wait_ge(qt_done, t - 1)
                else:
                    pe.wait_ge(tr_lo, 4 * NT)
                tbb = tb[t % 2][:, :].bitcast(BF16)
                for k in range(KT):
                    ins = pe.transpose(tbb[:, k * P:k * P + TP], Qb[t % 3][0:TP, k * P:(k + 1) * P], ident_b[0:TP, 0:TP])
                ins.then_inc(qt_ready, 1)
            transpose_q(0)
            transpose_q(1)
            pe.wait_ge(s_tern, 32)
            for t in range(NT):
                pe.wait_ge(qt_done, t + 1)
                for j in range(NH):
                    n4 = 2 * (t % 2) + j
                    if t >= 2:
                        pe.wait_ge(f_done, 2 * (t - 2) + j + 1)
                    for k in range(KT):
                        ins = pe.matmul(fb[n4][0:TP, :], qT[t % 2][:, k, :], tern_w[j][:, :, k, :],
                                        start=k == 0, stop=k == KT - 1)
                    ins.then_inc(f_ready, 1)
                if t + 2 < NT:
                    transpose_q(t + 2)

        @block.scalar
        def _(act):
            def tr_half(n, t, h):
                act.wait_ge(tr_ready, n + 1)
                act.activation(xt_hi[:, 4 * h:4 * h + 4, t * TP:(t + 1) * TP],
                               tb[h][:, 0:4 * TP].rearrange("p (k n) -> p k n", k=4), ACT.Copy).then_inc(tr_hi, 1)

            def w_split_hi(landed, s, k):
                act.wait_ge(w_landed[k % STG], landed)
                act.activation(w_hi[:, s, k, :], w_stage[:, k % STG, :], ACT.Copy).then_inc(w_hi_done, 1)

            def first_hi(k):
                act.wait_ge(w_first[k], 16)
                act.activation(w_hi[:, 0, k, :], first_stage[k], ACT.Copy).then_inc(w_hi_done, 1)

            def late(n, at):
                pairs = LOOPS[n][3]
                return LOOPS[n][4] == 1 and not (n == 4 and at >= NT) and at + 1 < 2 * NT and pairs[at + 1] > 0

            def take(count, ready, b, used=True):
                act.wait_ge(y_ready, ready)
                if used:
                    act.wait_ge(y_stored[b], (count - b) * 8)
                act.activation(evict[0:TP, b, :], yb[b][0:TP, :], ACT.Copy).then_inc(y_free, 1)

            def sqrt_group(g):
                t0, t1 = LN_GROUPS[g]
                act.wait_ge(sd_ready, g + 1)
                act.activation(mv[0:TP, t0:t1, 1], mv[0:TP, t0:t1, 1], ACT.Sqrt).then_inc(sd_done, 1)

            act.sem_inc(y_free, 2)
            for k in range(3):
                first_hi(k)
            sqrt_group(0)
            for k in range(3, 6):
                first_hi(k)
            for h in range(2):
                tr_half(h, 0, h)
            for k in range(6, KT):
                first_hi(k)

            for n, (first, iters, units, pairs, half) in enumerate(LOOPS):
                with loop(act, iters) as i:
                    for s in range(units):
                        u = i * units + (first + s)
                        for m in range(NT):
                            if n == 0 and s == 0:
                                for k in range(KT):
                                    if (m, k) in TRANSPOSE_AT:
                                        t = TRANSPOSE_AT[m, k]
                                        for h in range(2):
                                            tr_half(2 * t + h, t, h)
                                if m in (0, 3):
                                    sqrt_group(1 if m == 0 else 2)
                            def next_weights():
                                if 1 <= m <= KT:
                                    k = m - 1
                                    if k == 0 and first + s > 0:
                                        act.wait_ge(y_ready, u * NT)
                                    w_split_hi(u * 32 + 16 * (k // STG + 1), (s + 1) % 2, k)
                            if not with_pairs(n, s, m):
                                next_weights()
                            for p in with_pairs(n, s, m):
                                q = before(n) + p
                                for e in range(2):
                                    s6 = 2 * (q % AHEAD) + e
                                    landed = i * (16 * sum(pairs) // AHEAD) + 16 * (q // AHEAD + 1)
                                    act.wait_ge(g_landed[s6], landed + 16 * half * CHX // GS)
                                    if half == 0:
                                        act.wait_ge(gw_landed[s6], landed)
                                        scale = w_slot[:, s6, :]
                                    else:
                                        scale = w_all[:, bass.ds(i * (2 * sum(pairs)) + (2 * q + e), 1)]
                                    act.wait_ge(agg_mm, i * (2 * sum(pairs)) + (2 * q + e + half * CH + 1))
                                    act.activation(msg_hi[:, e, :], gslot[s6], ACT.Copy, scale=scale).then_inc(msg_hi_done, 1)
                                if p == with_pairs(n, s, m)[0]:
                                    if s * NT + m > 0 and late(n, s * NT + m - 1):
                                        take(stored(u) + m - 1, u * NT + m, (m - 1) % 2)
                                    next_weights()
                            if (n, s) != (4, 1) and not late(n, s * NT + m):
                                if n == 0 and s == 0 and m == 0:
                                    act.wait_ge(w_lo_done, 4)
                                take(stored(u) + m, u * NT + (m + 1), m % 2, n > 0 or s > 0 or m > 1)
                            if (n, s) == (5, 1) and m in (7, 8):
                                for h in range(2):
                                    tr_half(2 * NT + 2 * (m - 7) + h, m - 7, h)
                            if n == 1 and s == 1 and m < KT:
                                act.wait_ge(tern_t, m + 1)
                                if m >= 2:
                                    act.wait_ge(tern_st[m % 2], 16 * (m // 2))
                                act.activation(tern_out[m % 2], tb[m % 2][:, :].bitcast(BF16), ACT.Copy
                                               ).then_inc(tern_c, 1)
            def tanh_u(t):
                s = t % 2
                if t >= 2:
                    act.wait_ge(y2_ready, 2 * (t - 1))
                    act.wait_ge(a_in[s], 16 * (t // 2))
                    act.activation(Rr[s][0:TP, :], A[s][0:TP, :], ACT.Tanh).then_inc(th_done, 1)
                else:
                    act.wait_ge(ur_out, 16)
                    for h, part in enumerate((U_left[t][0:TP, :], agg[0:TP, t, :])):
                        ins = act.activation(Rr[s][0:TP, h * H:(h + 1) * H], part, ACT.Tanh)
                    ins.then_inc(th_done, 1)

            def norm_x(t):
                s = t % 2
                act.wait_ge(th_done, t + 1)
                act.wait_ge(x_in[s], 16 * (t // 2 + 1))
                act.wait_ge(s_nm, 1)
                act.activation(A[s][0:TP, :], Xx[s][0:TP, :], ACT.Identity, bias=nmean[0:TP, t:t + 1],
                               scale=mv[0:TP, t, 1:2])
                act.activation(Xx[s][0:TP, :], Xx[s][0:TP, :], ACT.Identity, bias=nmean[0:TP, t:t + 1],
                               scale=one_rstd[0:TP, t:t + 1]).then_inc(xl2_ready, 1)
            act.wait_ge(y_ready, 20 * NT)
            for t in (2, 3):
                for h in range(2):
                    tr_half(2 * NT + 2 * t + h, t, h)
            tanh_u(0)
            tanh_u(1)
            norm_x(0)
            for k in range(KT):
                w_split_hi(16 * (20 * 2 + k // STG + 1), 1, k)
            norm_x(1)
            for t in range(NT):
                act.wait_ge(sd_ready, len(LN_GROUPS) + t + 1)
                act.activation(sm[0:TP, 0:1], sm[0:TP, 0:1], ACT.Sqrt).then_inc(sd_done, 1)
                if t + 2 < NT:
                    tanh_u(t + 2)
                    if t >= 2:
                        for h in range(2):
                            tr_half(2 * NT + 2 * (t + 2) + h, t + 2, h)
                    norm_x(t + 2)
            for q in range(2):
                act.wait_ge(gate_ready[q], NT)
                act.wait_ge(xn_out[q], 16 * (NT // 2 - 1))
            for v in range(2, NT):
                act.dma_start(Xe[v][0:TP, :], rows(xn_dram, E_ORDER[v])).then_inc(xe_in[v], 16)
            for t in range(NT):
                act.wait_ge(qt_ready, t + 1)
                if t >= 2:
                    act.wait_ge(f_ready, 2 * (t - 1))
                act.activation(qT[t % 2], tb[t % 2][:, :].bitcast(BF16).rearrange("p (k n) -> p k n", k=KT)[:, :, 0:TP],
                               ACT.Copy).then_inc(qt_done, 1)
        @block.vector
        def _(dve):
            steps = [0]

            def done(ins):
                steps[0] += 1
                ins.then_inc(s_dve, 1)
                dve.wait_ge(s_dve, steps[0])

            dve.sem_inc(agg_added, MB)

            def row_stats(tile, mean_var, wait=True):
                for h in range(2):
                    done(dve.bn_stats(stats[0:TP, h, :], tile[:, h * H:(h + 1) * H]))
                done(dve.bn_aggr(mean_var, stats[0:TP, 0:2, :].rearrange("p a b -> p (a b)")))

            def normalise(t):
                dve.tensor_scalar(XA[t][0:TP, :], XA[t][0:TP, :], mv[0:TP, t, 0:1], mv[0:TP, t, 1:2], ALU.subtract, ALU.mult
                                  ).then_inc(xl_ready, 1)

            def statistics(t):
                dve.wait_ge(s_x[t], 16)
                row_stats(XA[t][0:TP, :], mv[0:TP, t, :])

            def roots(g):
                t0, t1 = LN_GROUPS[g]
                dve.tensor_scalar(mv[0:TP, t0:t1, 1], mv[0:TP, t0:t1, 1], LN_EPS, None, ALU.add).then_inc(sd_ready, 1)
                dve.wait_ge(sd_done, g + 1)
                done(dve.reciprocal(mv[0:TP, t0:t1, 1], mv[0:TP, t0:t1, 1]))
                for t in range(t0, t1):
                    normalise(t)

            def split_x(t):
                lo_half(dve, 2 * t, t)

            for t in range(2):
                statistics(t)
            roots(0)
            for t in range(2):
                split_x(t)
            for t in range(2, 5):
                statistics(t)
            roots(1)
            split_x(2)
            statistics(5)
            statistics(6)
            split_x(3)
            statistics(7)
            statistics(8)
            split_x(4)
            statistics(9)
            roots(2)
            for t in range(5, NT):
                split_x(t)

            dve.wait_ge(s_edges, 48)
            done(dve.tensor_copy(srcf, ei[0]))
            done(dve.tensor_copy(dstf, ei[1]))
            done(dve.tensor_scalar(tile_a, dstf, float(TP), None, ALU.is_ge))
            cur, nxt = tile_a, tile_b
            for t in range(2, NT):
                done(dve.scalar_tensor_tensor(nxt, dstf, float(t * TP), cur, ALU.is_ge, ALU.add))
                cur, nxt = nxt, cur
            tl = cur
            done(dve.scalar_tensor_tensor(lowf, tl, -float(TP), dstf, ALU.mult, ALU.add))
            for t in range(NT):
                ins = dve.tensor_scalar(oh_t[:, t * EC:(t + 1) * EC], tl, float(t), None, ALU.is_equal)
            ins.then_inc(oh_tile, 1)
            done(dve.tensor_copy(typf, ex[11].bitcast(I32)))
            done(dve.scalar_tensor_tensor(k80, tl, float(R), typf, ALU.mult, ALU.add))
            done(dve.scalar_tensor_tensor(bfld, typf, float(P), lowf, ALU.mult, ALU.add))
            done(dve.tensor_scalar(bfld, bfld, 1.0, None, ALU.add))
            for o in range(KT):
                dve.wait_ge(s_wf[o % 2], 16 * (o // 2 + 1))
                dve.tensor_reduce(asum[:, o:o + 1], T[o % 2], AX.X, ALU.add, apply_absolute_value=True).then_inc(wf_used, 1)
            dve.wait_ge(wf_used, KT)
            done(dve.tensor_reduce(tot_s, asum[:, 0:KT], AX.X, ALU.add))
            dve.memset(tot_n, 0.0).then_inc(part_in, 1)
            w2 = 2 * EC
            for q in range(NT // 2):
                for n, dest, m in ((2 * q, cumT, P), (2 * q + 1, rankV, TP)):
                    dve.wait_ge(rank_ready, n + 1)
                    dve.tensor_copy(dest[:, q * w2:(q + 1) * w2], ab[n % 2][0:m, 0:w2]).then_inc(rank_used, 1)
            dve.wait_ge(rank_used, NT)
            done(dve.tensor_tensor(rankV, rankV, cumT[0:TP, :], ALU.subtract))
            done(dve.memset(cumI, 0.0))
            done(dve.tensor_tensor_scan(cumI, cumI, cumT, 0.0, ALU.add, ALU.add))
            done(dve.tensor_tensor(rankV, rankV, cumI[0:TP, :], ALU.add))
            ends = cumI.rearrange("p (t c) -> p t c", t=NT)[:, :, EC - 1]
            done(dve.tensor_copy(tmp10, ends))
            done(dve.tensor_copy(cntt[:, 0:1], tmp10[:, 0:1]))
            done(dve.tensor_tensor(cntt[:, 1:NT], tmp10[:, 1:NT], tmp10[:, 0:NT - 1], ALU.subtract))
            done(dve.tensor_scalar(cap_i.bitcast(I32), cntt, float(2 * P - 1), None, ALU.add))
            done(dve.tensor_scalar(cap_i.bitcast(I32), cap_i.bitcast(I32), -2 * P, None, ALU.bitwise_and))
            done(dve.tensor_copy(capt, cap_i.bitcast(I32)))
            done(dve.memset(base, 0.0))
            done(dve.tensor_tensor_scan(base, base, capt, 0.0, ALU.add, ALU.add))
            done(dve.tensor_tensor(base, base, capt, ALU.subtract))
            done(dve.tensor_tensor(delta_t, base, tmp10, ALU.subtract))
            done(dve.tensor_tensor(delta_t, delta_t, cntt, ALU.add))
            v3 = rankV.rearrange("p (t c) -> p t c", t=NT)
            o3 = oh_t.rearrange("p (t c) -> p t c", t=NT)
            done(dve.tensor_tensor(v3, v3, delta_t[0:TP, :].unsqueeze(2).to_broadcast([TP, NT, EC]), ALU.add))
            done(dve.tensor_tensor(rankV, rankV, oh_t, ALU.mult))
            done(dve.tensor_reduce(pcf, rankV.rearrange("p (t c) -> p c t", t=NT), AX.X, ALU.add))
            pos_i, lane_i = tile_a.bitcast(I32), tile_b.bitcast(I32)
            done(dve.tensor_copy(pos_i, pcf))
            done(dve.tensor_scalar(lane_i, pos_i, P - 1, None, ALU.bitwise_and))
            done(dve.tensor_copy(plf, lane_i))
            done(dve.tensor_scalar(lane_i, pos_i, 7, None, ALU.arith_shift_right))
            done(dve.tensor_copy(pcf, lane_i))
            ca, cb = cumT[:, 0:CHX], cumT[:, CHX:2 * CHX]
            i128 = cumT[:, 2 * CHX:2 * CHX + CH]
            done(dve.tensor_scalar(i128, iota[:, :], float(P), None, ALU.mult))
            done(dve.memset(ca, float(NT - 1)))
            done(dve.memset(cb, float(NT - 1)))
            done(dve.tensor_scalar(ca[:, 0:CH], i128, base[:, 1:2], None, ALU.is_ge))
            for t in range(2, NT):
                done(dve.scalar_tensor_tensor(cb[:, 0:CH], i128, base[:, t:t + 1], ca[:, 0:CH], ALU.is_ge, ALU.add))
                ca, cb = cb, ca
            done(dve.tensor_copy(tile_i[0:1, :], ca[0:1, :].rearrange("o (c e) -> o c e", e=2)[:, :, 0]))
            dve.tensor_scalar(low_s[:, :], ca, float(R), None, ALU.mult).then_inc(scratch_free, 1)

            dve.wait_ge(part_out, 1)
            done(dve.tensor_scalar(thr, psums[:, 0:1], 1.0 / (D * D), None, ALU.mult))
            done(dve.tensor_scalar(thr, thr, 0.7, None, ALU.mult))
            done(dve.tensor_scalar(nthr, thr, -1.0, None, ALU.mult))
            for o in range(KT):
                dve.wait_ge(s_wf[o % 2], 16 * (KT // 2 + o // 2 + 1))
                w = T[o % 2]
                done(dve.tensor_scalar(G2b, w, nthr, None, ALU.is_lt))
                dve.scalar_tensor_tensor(tern_v[o], w, thr, G2b, ALU.is_gt, ALU.subtract).then_inc(tern_ready, 1)
                dve.wait_ge(tern_ready, o + 1)
                done(dve.scalar_tensor_tensor(G2b, w, 1.0, tern_v[o], ALU.mult, ALU.mult, accum_out=asum[:, o:o + 1]))
                dve.scalar_tensor_tensor(G2b, tern_v[o], 1.0, tern_v[o], ALU.mult, ALU.mult,
                                         accum_out=asum[:, KT + o:KT + o + 1]).then_inc(wf_used, 1)
                dve.wait_ge(wf_used, KT + o + 1)
            done(dve.tensor_reduce(tot_s, asum[:, 0:KT], AX.X, ALU.add))
            dve.tensor_reduce(tot_n, asum[:, KT:2 * KT], AX.X, ALU.add).then_inc(part_in, 1)

            for q in range(2):
                dve.wait_ge(tern_st[q], 16 * KT // 2)
            dve.sem_inc(oh_used, 2)

            def bc(ap, w):
                return ap.unsqueeze(2).to_broadcast([TP, NB, w])

            def io(w):
                return iota[0:TP, 0:w].unsqueeze(1).to_broadcast([TP, NB, w])

            with dve.Fori(0, 2) as i:
                for b20 in range(EC // NB // 2):
                    b = i * (EC // NB // 2) + b20
                    ohl, rhs, eq, ohlow, oh80 = batches[b20 % 2]
                    cols = lambda ap: ap[:, bass.ds(b * NB, NB)]
                    dve.wait_ge(oh_used, b + 1)
                    dve.tensor_tensor(eq, io(CH), bc(cols(pcf), CH), ALU.is_equal).then_inc(eq_ready, 1)
                    dve.tensor_tensor(ohl, io(P), bc(cols(plf), P), ALU.is_equal)
                    dve.tensor_tensor(ohlow, io(P), bc(cols(lowf), P), ALU.is_equal)
                    dve.tensor_tensor(oh80, io(NT * R), bc(cols(k80), NT * R), ALU.is_equal)
                    dve.wait_ge(eq_ready, b + 1)
                    dve.tensor_tensor(rhs[:, :, 0:CH], eq, bc(cols(srcf), CH), ALU.mult)
                    dve.tensor_tensor(rhs[:, :, CH:2 * CH], eq, bc(cols(bfld), CH), ALU.mult).then_inc(oh_ready, 1)

            dve.wait_ge(oh_used, EC // NB + 2)
            sv = big[:, 0:4 * CH].rearrange("p (a c) -> p a c", a=4)
            tabs = big[:, 2048:2048 + NT * R]
            tabs2 = big[:, 2560:2560 + CH]
            ti = sv[:, 2, :].bitcast(I32)
            tj = sv[:, 3, :].bitcast(I32)
            done(dve.memset(tabs, 0.0))
            done(dve.tensor_scalar(tabs[0:TP, :], cnt_b[0:TP, 0:NT * R], 1.0, None, ALU.max))
            dve.reciprocal(tabs[0:TP, :], tabs[0:TP, :]).then_inc(idx_ready, 1)
            done(dve.tensor_scalar(ti, perm_b[:, CH:2 * CH], -1.0, None, ALU.add))
            done(dve.tensor_scalar(tj, ti, P - 1, None, ALU.bitwise_and))
            low = tabs2
            done(dve.tensor_copy(low, tj))
            done(dve.tensor_scalar(tj, ti, 7, None, ALU.arith_shift_right))
            done(dve.tensor_copy(sv[:, 0, :], tj))
            done(dve.tensor_scalar(sv[:, 0, :], sv[:, 0, :], 0.0, None, ALU.max))
            done(dve.scalar_tensor_tensor(idx_all[:, 0, 0:CH], sv[:, 0, :], float(N), perm_b[:, 0:CH], ALU.mult, ALU.add))
            done(dve.scalar_tensor_tensor(sv[:, 1, :], low, float(NT * R), sv[:, 0, :], ALU.mult, ALU.add))
            done(dve.tensor_tensor(idx_all[:, 1, 0:CH], sv[:, 1, :], low_s[:, 0:CH], ALU.add))
            dve.tensor_copy(low_s[:, 0:CH], low).then_inc(idx_ready, 1)

            def split(c, at, half):
                e, s6, n = at % 2, at % GS, c + half * CH
                factor = w_slot[:, s6, :] if half == 0 else w_all[:, bass.ds(c, 1)]
                dve.wait_ge(agg_mm, n + 1)
                dve.tensor_scalar(onehot[:, e, 0:TP], iota[:, 0:TP], low_s[:, bass.ds(c, 1)], None, ALU.is_equal)
                dve.wait_ge(msg_hi_done, n + 1)
                dve.scalar_tensor_tensor(msg_lo[:, e, :], gslot[s6], factor, f(msg_hi[:, e, :]),
                                         ALU.mult, ALU.subtract).then_inc(msg_lo_done, 1)
                if half == 0:
                    dve.tensor_copy(w_all[:, bass.ds(c, 1)], w_slot[:, s6, :]).then_inc(w_kept, 1)

            def add(p, at, half):
                v = dve.value_load(tile_i[0:1, bass.ds(p, 1)], min_val=0, max_val=NT - 1)
                dve.wait_ge(agg_mm, 2 * p + (2 * half * PAIRS + 4))
                dve.wait_ge(agg_added, p + (half * PAIRS + MB))
                acc = agg[0:TP, bass.ds(v, 1), :]
                dve.tensor_tensor(acc, acc, mb[at % MB][0:TP, :].unsqueeze(1), ALU.add).then_inc(agg_added, 1)

            def step(p, at, half):
                for e in range(2):
                    split(2 * p + (2 + e), 2 * at + 2 + e, half)
                add(p, at, half)

            def edges(first, last, half):
                n = (last - first - (last == PAIRS)) // AHEAD
                if n > 1:
                    with dve.Fori(0, n) as i:
                        for j in range(AHEAD):
                            step(i * AHEAD + (first + j), first + j, half)
                    first += n * AHEAD
                for p in range(first, last):
                    if p + 1 < PAIRS:
                        step(p, p, half)
                    else:
                        add(p, p, half)

            dve.wait_ge(idx_ready, 2)
            for half in range(NH):
                if half == 0:
                    first, iters, units, pairs, _ = LOOPS[3]
                    with dve.Fori(0, iters) as i:
                        for s in range(units):
                            for m in range(NT):
                                for p in with_pairs(3, s, m):
                                    c = 2 * (i * sum(pairs) + p)
                                    if p == 0:
                                        split(c, 0, 0)
                                        split(c + 1, 1, 0)
                                        dve.wait_ge(agg_set, 16)
                                    if p + 1 < sum(pairs):
                                        step(i * sum(pairs) + p, p, 0)
                                    else:
                                        add(i * sum(pairs) + p, p, 0)
                                if 1 <= m <= KT:
                                    g = (i * units + (first + s)) * KT + (KT + m)
                                    dve.wait_ge(w_hi_done, g)
                                    dve.wait_ge(w_lo_done, g - 1)
                                    dve.tensor_tensor(w_lo[:, (s + 1) % 2, m - 1, :], w_stage[:, (m - 1) % STG, :],
                                                      f(w_hi[:, (s + 1) % 2, m - 1, :]), ALU.subtract).then_inc(w_lo_done, 1)
                    continue
                split(0, 0, 1)
                split(1, 1, 1)
                dve.wait_ge(agg_set, 32)
                at = sum(pairs_c1[:NT])
                edges(0, at, 1)
                for m in range(NT):
                    edges(at, at + pairs_c1[NT + m], 1)
                    at += pairs_c1[NT + m]
                    dve.wait_ge(y_ready, ROOT_R * NT + m + 1)
                    dve.wait_ge(agg_added, PAIRS + at + MB)
                    dve.tensor_tensor(agg[0:TP, m, :], yb[m % 2][0:TP, :], agg[0:TP, m, :], ALU.add).then_inc(root_added, 1)
                    dve.wait_ge(root_added, m + 1)
                edges(at, PAIRS, 1)

            done(dve.tensor_tensor(nmean[0:TP, :], mv[0:TP, :, 0], mv[0:TP, :, 1], ALU.mult))
            done(dve.tensor_scalar(one_rstd[0:TP, :], mv[0:TP, :, 1], 1.0, None, ALU.add))
            dve.tensor_scalar(nmean[0:TP, :], nmean[0:TP, :], -1.0, None, ALU.mult).then_inc(s_nm, 1)
            for t in range(4):
                lo_half(dve, 2 * NT + 2 * t, t)
            for k in range(KT):
                dve.wait_ge(w_hi_done, 21 * KT + k + 1)
                dve.tensor_tensor(w_lo[:, 1, k, :], w_stage[:, k % STG, :], f(w_hi[:, 1, k, :]), ALU.subtract).then_inc(last_lo, 1)
            mvt = sm[0:TP, 2:4]
            for t in range(NT):
                s = t % 2
                r, z, xn = (b[s][0:TP, :] for b in (Rr, Zz, Xn))
                for j in range(NH):
                    zj, rj = (b[:, j * H:(j + 1) * H] for b in (z, r))
                    dve.wait_ge(gate_ready[j], t + 1)
                    dve.wait_ge(base_ready, 2 * t + j + 1)
                    dve.tensor_tensor(rj, gb[t % 2][j][0:TP, :], rj, ALU.mult).then_inc(gate_taken, 1)
                    dve.wait_ge(gate_taken, 2 * t + j + 1)
                    dve.tensor_tensor(zj, zj, rj, ALU.add).then_inc(y2_ready, 1)
                    dve.wait_ge(y2_ready, 2 * t + j + 1)
                    done(dve.bn_stats(stats[0:TP, j, :], zj))
                done(dve.bn_aggr(mvt, stats[0:TP, 0:2, :].rearrange("p a b -> p (a b)")))
                done(dve.tensor_scalar(sm[0:TP, 1:2], mvt[:, 1:2], LN_EPS, LN_EPS, ALU.add, ALU.mult))
                dve.tensor_tensor(sm[0:TP, 0:1], sm[0:TP, 1:2], mvt[:, 1:2], ALU.add).then_inc(sd_ready, 1)
                if t >= 2:
                    dve.wait_ge(xn_out[s], 16 * (t // 2))
                else:
                    dve.wait_ge(s_bc, 32)
                dve.scalar_tensor_tensor(xn, z, mvt[:, 0:1], X0[0:TP, :], ALU.subtract, ALU.mult).then_inc(n_ready, 1)
                dve.wait_ge(sd_done, len(LN_GROUPS) + t + 1)
                done(dve.reciprocal(sm[0:TP, 0:1], sm[0:TP, 0:1]))
                dve.wait_ge(n_ready, t + 1)
                dve.scalar_tensor_tensor(xn, xn, sm[0:TP, 0:1], X1[0:TP, :], ALU.mult, ALU.add).then_inc(xn_ready, 1)
                dve.wait_ge(xn_ready, t + 1)
                dve.tensor_reduce(amax[0:TP, t:t + 1], xn, AX.X, ALU.max, apply_absolute_value=True).then_inc(xn_maxed, 1)
                if 2 <= t < NT - 2:
                    lo_half(dve, 2 * NT + 2 * (t + 2), t + 2)
            dve.wait_ge(xn_maxed, NT)
            dve.tensor_reduce(gmx[0:TP, :], amax[0:TP, :], AX.X, ALU.max).then_inc(gm_in, 1)
            dve.wait_ge(part_out, 2)
            done(dve.tensor_scalar(tot_n, psums[:, 1:2], 1.0, None, ALU.max))
            done(dve.reciprocal(tot_n, tot_n))
            done(dve.tensor_tensor(alpha, psums[:, 0:1], tot_n, ALU.mult))
            dve.wait_ge(gm_out, 1)
            done(dve.tensor_scalar(gms[0:TP, :], gms[0:TP, :], 1e-8, 1.0 / 127.0, ALU.max, ALU.mult))
            done(dve.reciprocal(qinv[0:TP, :], gms[0:TP, :]))
            done(dve.tensor_tensor(outscale[0:TP, :], gms[0:TP, :], alpha[0:TP, :], ALU.mult))
            for t in range(NT + 2):
                if t < NT:
                    a = Xe[t][0:TP, :]
                    if t >= 2:
                        dve.wait_ge(xe_in[t], 16)
                    b = Qf[t % 2][0:TP, :]
                    done(dve.tensor_scalar(b, a, qinv[0:TP, :], 127.0, ALU.mult, ALU.min))
                    a = b
                    done(dve.tensor_scalar(a, a, -127.0, MAGIC, ALU.max, ALU.add))
                    if t >= 3:
                        dve.wait_ge(qt_ready, t - 2)
                    dve.tensor_scalar(Qb[t % 3][0:TP, :], a, -MAGIC, None, ALU.add).then_inc(q_ready, 1)
                if t >= 2:
                    m = t - 2
                    z = Ze[m][0:TP, :]
                    if m >= 2:
                        dve.wait_ge(ze_in[m], 16)
                    if m >= 4:
                        dve.wait_ge(o_out[m % 4], 16 * (m // 4))
                    for j in range(NH):
                        dve.wait_ge(f_ready, 2 * m + j + 1)
                        zj = z[:, j * H:(j + 1) * H]
                        oj = Oe[m % 4][0:TP, j * H:(j + 1) * H]
                        dve.scalar_tensor_tensor(oj, fb[2 * (m % 2) + j][0:TP, :], outscale[0:TP, :], zj, ALU.mult, ALU.add
                                                 ).then_inc(f_done, 1)

        @block.gpsimd
        def _(pool):
            pool.iota(iota[:, :], pattern=[[1, CH]], base=0, channel_multiplier=0,
                      allow_small_or_imprecise_dtypes=True).then_inc(s_const, 1)
            pool.memset(idx_all[:, :, :], 0).then_inc(s_const, 1)
            for m in (ident, ident_b):
                pool.memset(m[:, :], 1.0).then_inc(s_const, 1)
            pool.wait_ge(s_const, 4)
            pool.affine_select(out=ident[:, :], in_=ident[:, :], compare_op=ALU.is_equal, fill=0.0, base=0,
                               pattern=[[-1, P]], channel_multiplier=1)
            pool.affine_select(out=ident_b[:, :], in_=ident_b[:, :], compare_op=ALU.is_equal, fill=0.0, base=0,
                               pattern=[[-1, P]], channel_multiplier=1).then_inc(s_const, 1)
            pool.sem_inc(agg_mm, 2)

            def w_split_lo(done_hi, s, k):
                pool.wait_ge(w_hi_done, done_hi)
                pool.tensor_tensor(w_lo[:, s, k, :], w_stage[:, k % STG, :], f(w_hi[:, s, k, :]), ALU.subtract
                                   ).then_inc(w_lo_done, 1)

            for k in range(KT):
                pool.wait_ge(w_hi_done, k + 1)
                pool.tensor_tensor(w_lo[:, 0, k, :], first_stage[k], f(w_hi[:, 0, k, :]), ALU.subtract).then_inc(w_lo_done, 1)

            def triangles():
                pool.wait_ge(tr_lo, 2 * NT)
                pool.memset(ones_b, 1.0)
                pool.memset(low_tri, 1.0).then_inc(s_const, 1)
                pool.wait_ge(s_const, 6)
                pool.affine_select(out=low_tri, in_=low_tri, compare_op=ALU.is_gt, fill=0.0, base=0,
                                   pattern=[[1, 128]], channel_multiplier=-1).then_inc(s_const, 1)

            def load_ffn(o):
                if o >= 2:
                    pool.wait_ge(wf_used, o - 1)
                if o >= KT:
                    pool.wait_ge(scratch_free, 1)
                pool.dma_start(T[o % 2], wffn[(o % KT) * P:(o % KT + 1) * P, :]).then_inc(s_wf[o % 2], 16)

            def part_sum(n):
                pool.wait_ge(part_in, n + 1)
                pool.partition_all_reduce(psums[:, 0:2], both, P, bass.bass_isa.ReduceOp.add).then_inc(part_out, 1)

            def gather_pair(p, r3, half):
                pool.tensor_copy(idx_slot[:, r3, 0:2 - half, :], idx_all[:, 0:2 - half, bass.ds(p * 2, 2)]).then_inc(icopy, 1)
                pool.wait_ge(icopy, p + (half * CHX // 2 + 1))
                pool.sem_inc(icopy_seen, 1)
                for e in range(2):
                    s6 = 2 * r3 + e
                    if half == 0:
                        pool.indirect_dma_start(out=w_slot[:, s6, :], out_offset=None, in_=inv_dram,
                                                in_offset=bass.IndirectOffsetOnAxis(ap=idx_slot[:, r3, 1, e:e + 1], axis=0)
                                                ).then_inc(gw_landed[s6], 16)
                    pool.indirect_dma_start(out=gslot[s6], out_offset=None, in_=y_dram[half],
                                            in_offset=bass.IndirectOffsetOnAxis(ap=idx_slot[:, r3, 0, e:e + 1], axis=0)
                                            ).then_inc(g_landed[s6], 16)

            def set_agg(half):
                pool.dma_start(agg[0:TP, :, :], bias[half * H:(half + 1) * H].unsqueeze(0).unsqueeze(0).to_broadcast([TP, NT, H])
                               ).then_inc(agg_set, 16)

            for n, (first, iters, units, pairs, half) in enumerate(LOOPS):
                if n == 3:
                    pool.wait_ge(idx_ready, 1)
                    pool.dma_start(inv_dram.rearrange("(p c) o -> p (c o)", p=P), big[:, 2048:2048 + NT * R]).then_inc(s_inv, 16)
                    pool.wait_ge(s_inv, 16)
                    pool.wait_ge(idx_ready, 2)
                    set_agg(0)
                if n == 4:
                    pool.wait_ge(agg_added, PAIRS + MB)
                    pool.dma_start(agg_dram.rearrange("(t p) c -> p t c", p=TP), agg[0:TP, :, :]).then_inc(agg_out, 16)
                    pool.wait_ge(agg_out, 16)
                    set_agg(1)
                    pool.wait_ge(w_kept, CH)
                    for q in range(GS):
                        pool.wait_ge(g_landed[q], 16 * CHX // GS)
                        pool.wait_ge(gw_landed[q], 16 * CHX // GS)
                if n in (3, 4):
                    for q in range(2):
                        pool.wait_ge(y_stored[q], 16 * (half + 1) * R * NT // 2)
                    for p in range(AHEAD):
                        gather_pair(p, p, half)
                with loop(pool, iters) as i:
                    for s in range(units):
                        u = i * units + (first + s)
                        for m in range(NT):
                            for p in with_pairs(n, s, m):
                                q = before(n) + p
                                if half == 1 and q + AHEAD >= PAIRS:
                                    continue
                                pool.wait_ge(msg_lo_done, i * (2 * sum(pairs)) + (2 * (q + 1) + half * CH))
                                if half == 0:
                                    pool.wait_ge(w_kept, i * (2 * sum(pairs)) + 2 * (q + 1))
                                gather_pair(i * sum(pairs) + (q + AHEAD), q % AHEAD, half)
                            if 1 <= m <= KT and n != 3:
                                pool.wait_ge(w_lo_done, u * KT + (KT + m - 1))
                                w_split_lo(u * KT + (KT + m), (s + 1) % 2, m - 1)
                            if (n, s, m) == (4, 1, 2):
                                for q in range(2):
                                    pool.wait_ge(y_stored[q], 16 * ROOT_R * NT // 2)
                                pool.dma_start(rz_dram[0:N, :], agg_dram, accum_op=ALU.add, max_dma_last_dim=4 * H
                                               ).then_inc(u_summed, 16)
                            if n == 0 and s == 0 and m == 7:
                                triangles()
                            if n == 0 and s == 0 and 6 <= m:
                                load_ffn(2 * m - 12)
                                load_ffn(2 * m - 11)
                            if n == 0 and (s, m) == (1, 2):
                                part_sum(0)
                            if n == 1 and s == 0 and m < KT:
                                load_ffn(KT + m)
                            if n == 1 and (s, m) == (1, NT - 1):
                                part_sum(1)
            for q in range(2):
                pool.wait_ge(y_stored[q], 8 * stored(20))
            pool.dma_start(EV[0:TP, :], bgate.unsqueeze(0).to_broadcast([TP, D])).then_inc(s_bg, 16)
            for t in range(NT):
                s = t % 2
                a, xx, r, z = (b[s][0:TP, :] for b in (A, Xx, Rr, Zz))
                pool.wait_ge(xl2_ready, t + 1)
                pool.tensor_tensor(r, r, a, ALU.subtract).then_inc(lnx_used, 1)
                for j in range(NH):
                    xj, rj, zj, bj = (b[:, j * H:(j + 1) * H] for b in (xx, r, z, EV[0:TP, :]))
                    n = 2 * t + j
                    if n == 0:
                        pool.wait_ge(s_bg, 16)
                    pool.wait_ge(z_in[s], 16 * (t // 2 + 1))
                    pool.tensor_tensor(zj, zj, bj, ALU.add).then_inc(base_step, 1)
                    pool.wait_ge(lnx_used, t + 1)
                    pool.wait_ge(base_step, 2 * n + 1)
                    pool.tensor_tensor(zj, zj, rj, ALU.mult).then_inc(base_step, 1)
                    pool.wait_ge(base_step, 2 * n + 2)
                    pool.tensor_tensor(zj, zj, xj, ALU.add).then_inc(base_ready, 1)
            pool.wait_ge(gm_in, 1)
            pool.partition_all_reduce(gms[0:TP, :], gmx[0:TP, :], TP, bass.bass_isa.ReduceOp.max).then_inc(gm_out, 1)


def kernel(**inputs):
    import numpy as np
    from concourse import bacc
    from concourse.bass_utils import run_bass_kernel_spmd

    a = {k: np.asarray(v) for k, v in inputs.items()}
    rel, root, wg = a["L0_gnn_weight"], a["L0_gnn_root"], a["L0_gnn_w_gate"]
    mats = [(rel[r], j) for j in range(NH) for r in range(R)]
    mats += [(m, j) for m in (root, wg[D:], wg[:D]) for j in range(NH)]
    wall = np.concatenate([m[:, j * H:(j + 1) * H] for m, j in mats], axis=0)
    arrays = {
        "x": a["x"], "src": a["src"], "dst": a["dst"], "edge_type": a["edge_type_8"], "weights": wall,
        "bias": a["L0_gnn_bias"], "b_gate": a["L0_gnn_b_gate"], "ffn_weight": a["L0_ffn_weight"],
        "ffn_gamma": a["L0_ffn_gamma"], "ffn_beta": a["L0_ffn_beta"],
    }
    arrays = {k: np.ascontiguousarray(v) for k, v in arrays.items()}
    nc = bacc.Bacc("TRN2", target_bir_lowering=False, num_devices=1)
    args = [nc.dram_tensor(f"in_{k}", v.shape, mybir.dt.from_np(v.dtype), kind="ExternalInput").ap()
            for k, v in arrays.items()]
    args.append(nc.dram_tensor("out_y", (N, D), F32, kind="ExternalOutput").ap())
    build(nc, *args)
    r = run_bass_kernel_spmd(nc, [{f"in_{k}": v for k, v in arrays.items()}], core_ids=[0])
    return r.results[0]["out_y"]
```
